# Optimizing a Trainium2 kernel written in Bass

```python
import numpy as np
import jax
import jax.numpy as jnp

def _softmax(x, axis=-1):
    return jax.nn.softmax(x, axis=axis)

def _gelu(x):
    return jax.nn.gelu(x, approximate=True)

def _silu(x):
    return jax.nn.silu(x)

def _sigmoid(x):
    return jax.nn.sigmoid(x)

def _layernorm(x, axis=-1, eps=1e-05):
    m = jnp.mean(x, axis=axis, keepdims=True)
    v = jnp.var(x, axis=axis, keepdims=True)
    return (x - m) / jnp.sqrt(v + eps)

def _scatter_add(tgt, idx, src, axis=0):
    return tgt.at[idx].add(src)

def _segment_sum(src, seg, n):
    return jax.ops.segment_sum(src, seg, n)
kernel_name = 'mk_sandwich_d2_jaxref_r8_893c63'

def setup_inputs(seed: int=0):
    np.random.seed(seed)
    _w = jnp.asarray

    def _L0_attn_setup():
        import jax, jax.numpy as jnp
        import numpy as np
        import math
        D_MODEL = 256
        D_STATE = 16
        DT_RANK = 64
        DT_MIN, DT_MAX, DT_FLOOR = (0.001, 0.1, 0.0001)

        def _selective_scan(x, dt, A, B, C):
            xs = (jnp.swapaxes(x, 0, 1), jnp.swapaxes(dt, 0, 1), jnp.swapaxes(B, 0, 1), jnp.swapaxes(C, 0, 1))
            h0 = jnp.zeros((x.shape[0], x.shape[2], A.shape[1]), dtype=x.dtype)

            def step(h, inp):
                x_t, dt_t, B_t, C_t = inp
                A_bar = jnp.exp(dt_t[..., None] * A)
                h = A_bar * h + dt_t[..., None] * B_t[:, None, :] * x_t[..., None]
                y_t = jnp.einsum('bdn,bn->bd', h, C_t)
                return (h, y_t)
            _, ys = jax.lax.scan(step, h0, xs)
            return jnp.swapaxes(ys, 0, 1)
        key = jax.random.key(seed)
        k_x, k_xp, k_dtw, k_dtb = jax.random.split(key, 4)
        x = jax.random.normal(k_x, (4, 512, D_MODEL), dtype=jnp.float32)
        A_log = jnp.log(jnp.arange(1, D_STATE + 1, dtype=jnp.float32))[None, :].repeat(D_MODEL, axis=0)
        D = jnp.ones((D_MODEL,), dtype=jnp.float32)
        W_xproj = jax.random.normal(k_xp, (DT_RANK + 2 * D_STATE, D_MODEL), dtype=jnp.float32) / math.sqrt(D_MODEL)
        W_dt = jax.random.normal(k_dtw, (D_MODEL, DT_RANK), dtype=jnp.float32) / math.sqrt(DT_RANK)
        dt = jnp.exp(jax.random.uniform(k_dtb, (D_MODEL,)) * (math.log(DT_MAX) - math.log(DT_MIN)) + math.log(DT_MIN))
        dt = jnp.clip(dt, DT_FLOOR, None)
        b_dt = dt + jnp.log(-jnp.expm1(-dt))
        return {'x': x, 'A_log': A_log, 'D': D, 'W_xproj': W_xproj, 'W_dt': W_dt, 'b_dt': b_dt}
    _L0_attn_in = _L0_attn_setup()

    def _L0_ffn_setup():
        import jax, jax.numpy as jnp
        import numpy as np
        D_IN = 256
        D_OUT = 256
        LN_EPS = 1e-05
        key = jax.random.key(seed)
        kx, kw, kb = jax.random.split(key, 3)
        x = jax.random.normal(kx, (8, 256, D_IN), dtype=jnp.float32)
        gamma = jnp.ones((D_IN,), dtype=jnp.float32)
        beta = jnp.zeros((D_IN,), dtype=jnp.float32)
        weight = jax.random.uniform(kw, (D_OUT, D_IN), dtype=jnp.float32) * 0.001
        bias = jax.random.uniform(kb, (D_OUT,), dtype=jnp.float32) * 0.001
        alpha = jnp.ones((D_OUT,), dtype=jnp.float32)
        return {'x': x, 'gamma': gamma, 'beta': beta, 'weight': weight, 'bias': bias, 'alpha': alpha}
    _L0_ffn_in = _L0_ffn_setup()

    def _L1_attn_setup():
        import jax, jax.numpy as jnp
        import numpy as np
        D_INNER = 256
        DT_RANK = 128
        D_STATE = 16

        def _softplus_thresh(x, threshold=20.0):
            return jnp.where(x > threshold, x, jax.nn.softplus(x))
        key = jax.random.key(seed)
        ks = jax.random.split(key, 8)
        B, L = (2, 128)
        x = jax.random.normal(ks[0], (B, L, D_INNER), dtype=jnp.float32)
        W_delta = jax.random.normal(ks[1], (D_INNER, DT_RANK), dtype=jnp.float32) * D_INNER ** (-0.5)
        W_B = jax.random.normal(ks[2], (D_INNER, D_STATE), dtype=jnp.float32) * D_INNER ** (-0.5)
        W_C = jax.random.normal(ks[3], (D_INNER, D_STATE), dtype=jnp.float32) * D_INNER ** (-0.5)
        W_dt = jax.random.normal(ks[4], (DT_RANK, D_INNER), dtype=jnp.float32) * DT_RANK ** (-0.5)
        b_dt = jax.random.normal(ks[5], (D_INNER,), dtype=jnp.float32) * 0.1
        A_log = jnp.log(jnp.broadcast_to(jnp.arange(1, D_STATE + 1, dtype=jnp.float32), (D_INNER, D_STATE)))
        D_param = jnp.ones((D_INNER,), dtype=jnp.float32)
        return {'x': x, 'W_delta': W_delta, 'W_dt': W_dt, 'b_dt': b_dt, 'W_B': W_B, 'W_C': W_C, 'A_log': A_log, 'D': D_param}
    _L1_attn_in = _L1_attn_setup()

    def _L1_ffn_setup():
        import jax, jax.numpy as jnp
        import numpy as np
        DIM = 256
        INTER = 176
        N_EXPERTS = 16
        TOP_K = 2
        N_SHARED = 2
        SHARED_INTER = N_SHARED * INTER

        def _swiglu(t, wa, wb, wo):
            h = jax.nn.silu(t @ wa.T) * (t @ wb.T)
            return h @ wo.T
        key = jax.random.key(seed)
        ks = jax.random.split(key, 9)
        s = 0.02
        return {'x': jax.random.normal(ks[0], (4, 256, DIM), dtype=jnp.float32), 'gate_w': jax.random.normal(ks[1], (N_EXPERTS, DIM), dtype=jnp.float32) * s, 'w1': jax.random.normal(ks[2], (N_EXPERTS, INTER, DIM), dtype=jnp.float32) * s, 'w2': jax.random.normal(ks[3], (N_EXPERTS, DIM, INTER), dtype=jnp.float32) * s, 'w3': jax.random.normal(ks[4], (N_EXPERTS, INTER, DIM), dtype=jnp.float32) * s, 'sw1': jax.random.normal(ks[5], (SHARED_INTER, DIM), dtype=jnp.float32) * s, 'sw2': jax.random.normal(ks[6], (DIM, SHARED_INTER), dtype=jnp.float32) * s, 'sw3': jax.random.normal(ks[7], (SHARED_INTER, DIM), dtype=jnp.float32) * s}
    _L1_ffn_in = _L1_ffn_setup()
    _d = {'L0_attn_x': _L0_attn_in['x'], 'L0_attn_A_log': _L0_attn_in['A_log'], 'L0_attn_D': _L0_attn_in['D'], 'L0_attn_W_xproj': _L0_attn_in['W_xproj'], 'L0_attn_W_dt': _L0_attn_in['W_dt'], 'L0_attn_b_dt': _L0_attn_in['b_dt'], 'L0_ffn_gamma': _L0_ffn_in['gamma'], 'L0_ffn_beta': _L0_ffn_in['beta'], 'L0_ffn_weight': _L0_ffn_in['weight'], 'L0_ffn_bias': _L0_ffn_in['bias'], 'L0_ffn_alpha': _L0_ffn_in['alpha'], 'L1_attn_W_delta': _L1_attn_in['W_delta'], 'L1_attn_W_dt': _L1_attn_in['W_dt'], 'L1_attn_b_dt': _L1_attn_in['b_dt'], 'L1_attn_W_B': _L1_attn_in['W_B'], 'L1_attn_W_C': _L1_attn_in['W_C'], 'L1_attn_A_log': _L1_attn_in['A_log'], 'L1_attn_D': _L1_attn_in['D'], 'L1_ffn_gate_w': _L1_ffn_in['gate_w'], 'L1_ffn_w1': _L1_ffn_in['w1'], 'L1_ffn_w2': _L1_ffn_in['w2'], 'L1_ffn_w3': _L1_ffn_in['w3'], 'L1_ffn_sw1': _L1_ffn_in['sw1'], 'L1_ffn_sw2': _L1_ffn_in['sw2'], 'L1_ffn_sw3': _L1_ffn_in['sw3']}
    _x0 = _d['L0_attn_x']
    _d['L0_attn_x'] = jax.random.normal(jax.random.fold_in(jax.random.key(seed), 1), (4, 512, 256), dtype=_x0.dtype)
    del _x0
    return _d

def reference(L0_attn_x, L0_attn_A_log, L0_attn_D, L0_attn_W_xproj, L0_attn_W_dt, L0_attn_b_dt, L0_ffn_gamma, L0_ffn_beta, L0_ffn_weight, L0_ffn_bias, L0_ffn_alpha, L1_attn_W_delta, L1_attn_W_dt, L1_attn_b_dt, L1_attn_W_B, L1_attn_W_C, L1_attn_A_log, L1_attn_D, L1_ffn_gate_w, L1_ffn_w1, L1_ffn_w2, L1_ffn_w3, L1_ffn_sw1, L1_ffn_sw2, L1_ffn_sw3):

    def _L0_attn_ref(x, A_log, D, W_xproj, W_dt, b_dt):
        import jax, jax.numpy as jnp
        import numpy as np
        import math
        D_MODEL = 256
        D_STATE = 16
        DT_RANK = 64
        DT_MIN, DT_MAX, DT_FLOOR = (0.001, 0.1, 0.0001)

        def _selective_scan(x, dt, A, B, C):
            xs = (jnp.swapaxes(x, 0, 1), jnp.swapaxes(dt, 0, 1), jnp.swapaxes(B, 0, 1), jnp.swapaxes(C, 0, 1))
            h0 = jnp.zeros((x.shape[0], x.shape[2], A.shape[1]), dtype=x.dtype)

            def step(h, inp):
                x_t, dt_t, B_t, C_t = inp
                A_bar = jnp.exp(dt_t[..., None] * A)
                h = A_bar * h + dt_t[..., None] * B_t[:, None, :] * x_t[..., None]
                y_t = jnp.einsum('bdn,bn->bd', h, C_t)
                return (h, y_t)
            _, ys = jax.lax.scan(step, h0, xs)
            return jnp.swapaxes(ys, 0, 1)
        A = -jnp.exp(A_log)
        x_proj = jnp.einsum('bld,ed->ble', x, W_xproj)
        dtp = x_proj[..., :DT_RANK]
        B = x_proj[..., DT_RANK:DT_RANK + D_STATE]
        C = x_proj[..., DT_RANK + D_STATE:]
        dt = jax.nn.softplus(jnp.einsum('blr,dr->bld', dtp, W_dt) + b_dt)
        y = _selective_scan(x, dt, A, B, C)
        return y + D * x

    def _L0_ffn_ref(x, gamma, beta, weight, bias, alpha):
        import jax, jax.numpy as jnp
        import numpy as np
        D_IN = 256
        D_OUT = 256
        LN_EPS = 1e-05
        mu = jnp.mean(x, axis=-1, keepdims=True)
        var = jnp.mean(jnp.square(x - mu), axis=-1, keepdims=True)
        xn = (x - mu) * jax.lax.rsqrt(var + LN_EPS) * gamma + beta
        a = jnp.sign(xn)
        centered = weight - jnp.mean(weight, axis=1, keepdims=True)
        signed_w = jnp.sign(centered)
        out = jnp.einsum('bsi,oi->bso', a, signed_w) + bias
        return out * alpha

    def _L1_attn_ref(x, W_delta, W_dt, b_dt, W_B, W_C, A_log, D):
        import jax, jax.numpy as jnp
        import numpy as np
        D_INNER = 256
        DT_RANK = 128
        D_STATE = 16

        def _softplus_thresh(x, threshold=20.0):
            return jnp.where(x > threshold, x, jax.nn.softplus(x))
        A = -jnp.exp(A_log)
        delta = _softplus_thresh(x @ W_delta @ W_dt + b_dt)
        Bp = x @ W_B
        Cp = x @ W_C
        abar = jnp.exp(delta[..., None] * A)
        bbar = delta[..., None] * Bp[:, :, None, :] * x[..., None]

        def combine(c1, c2):
            a1, b1 = c1
            a2, b2 = c2
            return (a1 * a2, a2 * b1 + b2)
        _, h = jax.lax.associative_scan(combine, (abar, bbar), axis=1)
        y = jnp.einsum('bldn,bln->bld', h, Cp) + x * D
        return y

    def _L1_ffn_ref(x, gate_w, w1, w2, w3, sw1, sw2, sw3):
        import jax, jax.numpy as jnp
        import numpy as np
        DIM = 256
        INTER = 176
        N_EXPERTS = 16
        TOP_K = 2
        N_SHARED = 2
        SHARED_INTER = N_SHARED * INTER

        def _swiglu(t, wa, wb, wo):
            h = jax.nn.silu(t @ wa.T) * (t @ wb.T)
            return h @ wo.T
        shape = x.shape
        t = x.reshape(-1, DIM)
        scores = jax.nn.softmax(t @ gate_w.T, axis=-1)
        weights, indices = jax.lax.top_k(scores, TOP_K)
        y = jnp.zeros_like(t)
        for e in range(N_EXPERTS):
            w_e = jnp.sum(jnp.where(indices == e, weights, 0.0), axis=-1)
            y = y + _swiglu(t, w1[e], w3[e], w2[e]) * w_e[:, None]
        z = _swiglu(t, sw1, sw3, sw2)
        return (y + z).reshape(shape)
    x = L0_attn_x
    x = x + _layernorm(_L0_attn_ref(_layernorm(x, axis=-1), L0_attn_A_log, L0_attn_D, L0_attn_W_xproj, L0_attn_W_dt, L0_attn_b_dt), axis=-1)
    x = x + _layernorm(_L0_ffn_ref(_layernorm(x, axis=-1), L0_ffn_gamma, L0_ffn_beta, L0_ffn_weight, L0_ffn_bias, L0_ffn_alpha), axis=-1)
    x = x + _layernorm(_L1_attn_ref(_layernorm(x, axis=-1), L1_attn_W_delta, L1_attn_W_dt, L1_attn_b_dt, L1_attn_W_B, L1_attn_W_C, L1_attn_A_log, L1_attn_D), axis=-1)
    x = x + _layernorm(_L1_ffn_ref(_layernorm(x, axis=-1), L1_ffn_gate_w, L1_ffn_w1, L1_ffn_w2, L1_ffn_w3, L1_ffn_sw1, L1_ffn_sw2, L1_ffn_sw3), axis=-1)
    return x

_drawn_inputs = setup_inputs


def setup_inputs(seed=0):
    import zlib

    import numpy as np

    out = dict(_drawn_inputs(seed))
    spreads = {'L0_attn_D': (1.0, 0.2),
     'L0_ffn_gamma': (1.0, 0.2),
     'L0_ffn_beta': (0.0, 0.1),
     'L0_ffn_alpha': (1.0, 0.2),
     'L1_attn_D': (1.0, 0.2)}
    factors = {}
    for name, (base, spread) in spreads.items():
        noise = np.random.default_rng([zlib.crc32(name.encode()), seed]).standard_normal(out[name].shape)
        drawn = base * np.exp(spread * noise) if base else spread * noise
        out[name] = jnp.asarray(drawn.astype(out[name].dtype))
    for name, factor in factors.items():
        out[name] = (out[name] * factor).astype(out[name].dtype)
    return out
```

```python
import concourse.bass as bass
from concourse import mybir
from contextlib import ExitStack

F32 = mybir.dt.float32
BF16 = mybir.dt.bfloat16
U32 = mybir.dt.uint32
ALU = mybir.AluOpType
ACT = mybir.ActivationFunctionType
AX = mybir.AxisListType

P = 128
D = 256
H = D // P
BATCH, SEQ = 4, 512
T = BATCH * SEQ
C = T // P
CQ = 4
Q = C // CQ
N = 16
RANK = (64, 128)
E = 16
ES = 18
INTER = 176
IR = INTER - P
EPS = 1e-5
UNITS = N * H
STATE_RING, ABAR_RING, CREP_RING = 8, 4, 4
REP = 3


def sandwich_kernel(nc, x, eye, a_log, d_skip, w_in, w_dt, b_dt, gamma, beta, weight, bias, alpha,
                    gate_wt, iota_e, w13, w2, out):
    ctx = ExitStack()
    with ctx:
        def sb(name, shape, dt=F32):
            return ctx.enter_context(nc.sbuf_tensor(name, shape, dt))

        def sem(name):
            return ctx.enter_context(nc.semaphore(name))

        X = sb("residual", [P, C, D])
        tok_a = sb("tok_a", [P, C, D])
        feat_a = sb("feat_a", [P, H, T])
        arena = sb("arena", [P, 3 * H * T // 1])
        dtT = arena[:, 0:H * T].rearrange("p (h t) -> p h t", h=H)
        uT = arena[:, H * T:2 * H * T].rearrange("p (h t) -> p h t", h=H)
        state = arena[:, 2 * H * T:2 * H * T + STATE_RING * SEQ].rearrange("p (r t) -> p r t", r=STATE_RING)
        w2a = arena[:, 0:ES * D].rearrange("p (e d) -> p e d", e=ES)
        w2b = arena[0:IR, ES * D:2 * ES * D].rearrange("p (e d) -> p e d", e=ES)
        yT = tok_a[:, :, :].rearrange("p c d -> p (c d)").rearrange("p (h t) -> p h t", h=H)
        f_tok = feat_a[:, :, :].rearrange("p h t -> p (h t)").rearrange("p (c d) -> p c d", c=C)
        abar = sb("abar", [P, ABAR_RING, SEQ])
        crep = sb("crep", [P, CREP_RING, SEQ])
        bcT = sb("bcT", [2 * N, T])
        dtpT = sb("dtpT", [P, T])
        w13_sb = sb("w13_sb", [P, H, ES, 2 * INTER])
        ident = sb("ident", [P, P])
        ident_bf = sb("ident_bf", [P, P], BF16)
        a_sb = [sb(f"a_sb{l}", [P, H, N]) for l in range(2)]
        dskip_sb = [sb(f"dskip_sb{l}", [P, H]) for l in range(2)]
        ddiag = sb("ddiag", [P, H, P])
        win_sb = [sb(f"win_sb{l}", [P, H, RANK[l] + 2 * N]) for l in range(2)]
        wdt_sb = [sb(f"wdt_sb{l}", [RANK[l], D]) for l in range(2)]
        bdt_sb = [sb(f"bdt_sb{l}", [P, H]) for l in range(2)]
        gamma_sb, beta_sb, bias_sb, alpha_sb = (sb(f"{n}_sb", [P, D]) for n in ("gamma", "beta", "bias", "alpha"))
        fw_sb = sb("fw_sb", [P, H, D])
        fw_sign = sb("fw_sign", [P, H, D], BF16)
        fw_signT = sb("fw_signT", [P, H, D], BF16)
        gatew_sb = sb("gatew_sb", [P, H, E])
        iota_sb = sb("iota_sb", [P, E])
        st6 = sb("st6", [P, C, 6])
        mom = sb("mom", [P, 6, C])
        std = sb("std", [P, C])
        rstd = sb("rstd", [P, C])
        probs = sb("probs", [P, C, E])
        psum_e = sb("psum_e", [P, C])
        top8 = sb("top8", [P, C, 8])
        top8i = sb("top8i", [P, C, 8], U32)
        top8f = sb("top8f", [P, C, 2])
        wsel = sb("wsel", [P, C, ES])
        wsel2 = sb("wsel2", [P, C, E])
        silu = sb("silu", [P, 2, INTER])
        gated = sb("gated", [P, 2, INTER])
        gatedT = sb("gatedT", [P, 2, 2, P])
        a_sign = arena[:, 0:H * T // 2].bitcast(BF16).rearrange("p (c d) -> p c d", c=C)
        a_signT = arena[:, H * T // 2:H * T].bitcast(BF16).rearrange("p (h t) -> p h t", h=H)

        bank = [ctx.enter_context(nc.psum_tensor(f"bank{i}", [P, 512], F32)) for i in range(8)]
        brep = [bank[0], bank[1], bank[6]]
        cps = [bank[2], bank[3], bank[7]]
        ysum = bank[4:6]
        work = bank[6:8]

        ld_x, ld_const, ld_ffn, ld_gate, ld_w13, ld_w2, stored = (
            sem(n) for n in ("ld_x", "ld_const", "ld_ffn", "ld_gate", "ld_w13", "ld_w2", "stored"))
        ld_ssm = [sem(f"ld_ssm{l}") for l in range(2)]
        dve_done = sem("dve_done")
        var_ready, std_ready = sem("var_ready"), sem("std_ready")
        norm_ready = sem("norm_ready")
        tr_ready, tr_copied = sem("tr_ready"), sem("tr_copied")
        proj_ready, proj_copied = sem("proj_ready"), sem("proj_copied")
        pre_ready, pre_used = sem("pre_ready"), sem("pre_used")
        exp_ready, w_ready, err_ready, ln_ready = (
            sem(n) for n in ("exp_ready", "w_ready", "err_ready", "ln_ready"))
        dt_ready = sem("dt_ready")
        a_exp_ready, a_ready, ddiag_ready = sem("a_exp_ready"), sem("a_ready"), sem("ddiag_ready")
        brep_ready, crep_ready, crep_copied = sem("brep_ready"), sem("crep_ready"), sem("crep_copied")
        abar_ready, b_ready, h_ready, hc_ready = (
            sem(n) for n in ("abar_ready", "b_ready", "h_ready", "hc_ready"))
        state_free = sem("state_free")
        ysum_free = sem("ysum_free")
        fsign_in, fsign_out, fwT_ready, fwT_copied = (
            sem(n) for n in ("fsign_in", "fsign_out", "fwT_ready", "fwT_copied"))
        xsign_in, xsign_out = sem("xsign_in"), sem("xsign_out")
        ffn_ready, ffn_used = sem("ffn_ready"), sem("ffn_used")
        gate_ready, sm_in, sm_out = sem("gate_ready"), sem("sm_in"), sem("sm_out")
        up_ready, silu_ready, gated_ready, gT_ready, gTa_copied, gTb_copied = (
            sem(n) for n in ("up_ready", "silu_ready", "gated_ready", "gT_ready", "gTa_copied", "gTb_copied"))
        route_ready, moe_ready, moe_copied = sem("route_ready"), sem("moe_ready"), sem("moe_copied")
        out_ready = sem("out_ready")

        block = ctx.enter_context(nc.Block())

        @block.sync
        def _(sp):
            sp.dma_start(X[:, :, :], x.rearrange("(c p) d -> p c d", p=P)).then_inc(ld_x, 16)
            sp.dma_start(ident[:, :], eye).then_inc(ld_const, 16)
            for l in range(2):
                for dst, src in ((a_sb[l], a_log[l]), (dskip_sb[l], d_skip[l]), (bdt_sb[l], b_dt[l])):
                    view = src.rearrange("(h p) n -> p h n", p=P) if dst is a_sb[l] else src
                    sp.dma_start(dst[:], view).then_inc(ld_ssm[l], 16)
                sp.dma_start(win_sb[l][:, :, :], w_in[l].rearrange("(h p) r -> p h r", p=P)).then_inc(ld_ssm[l], 16)
                sp.dma_start(wdt_sb[l][:, :], w_dt[l]).then_inc(ld_ssm[l], 16)
            sp.dma_start(fw_sb[:, :, :], weight.rearrange("(h p) d -> p h d", p=P)).then_inc(ld_ffn, 16)
            for dst, src in ((gamma_sb, gamma), (beta_sb, beta), (bias_sb, bias), (alpha_sb, alpha)):
                sp.dma_start(dst[:, :], src.partition_broadcast(P)).then_inc(ld_ffn, 16)
            sp.dma_start(gatew_sb[:, :, :], gate_wt.rearrange("(h p) e -> p h e", p=P)).then_inc(ld_gate, 16)
            sp.dma_start(iota_sb[:, :], iota_e.partition_broadcast(P)).then_inc(ld_gate, 16)
            for h in range(H):
                sp.dma_start(w13_sb[:, h], w13[:, h * P:(h + 1) * P, :].rearrange("e p i -> p e i")).then_inc(ld_w13, 16)
            sp.wait_ge(ysum_free, H + 2 * BATCH * H)
            sp.dma_start(w2a, w2[:, 0:P, :].rearrange("e p d -> p e d")).then_inc(ld_w2, 16)
            sp.dma_start(w2b, w2[:, P:INTER, :].rearrange("e p d -> p e d")).then_inc(ld_w2, 16)
            for q in range(Q):
                sp.wait_ge(out_ready, q + 1)
                sp.dma_start(out.rearrange("(c p) d -> p c d", p=P)[:, q * CQ:(q + 1) * CQ, :],
                             X[:, q * CQ:(q + 1) * CQ, :]).then_inc(stored, 16)
            sp.wait_ge(stored, 16 * Q)

        @block.vector
        def _(dve):
            steps = [0]
            norms = [0]

            def done(ins, times=1):
                steps[0] += times
                return ins.then_inc(dve_done, 1)

            def settle():
                dve.wait_ge(dve_done, steps[0])

            def moments(src):
                with dve.Fori(0, C) as c:
                    done(dve.bn_stats(st6[:, bass.ds(c, 1), :], src[:, bass.ds(c, 1), :]), 0)
                steps[0] += C
                settle()
                s = st6[:, :, :]
                done(dve.tensor_tensor(mom[:, 0, :], s[:, :, 1], s[:, :, 4], ALU.add))
                done(dve.tensor_tensor(mom[:, 1, :], s[:, :, 1], s[:, :, 4], ALU.subtract))
                done(dve.tensor_tensor(mom[:, 2, :], s[:, :, 2], s[:, :, 5], ALU.add))
                settle()
                done(dve.tensor_scalar(mom[:, 0, :], mom[:, 0, :], 0.5, None, ALU.mult))
                done(dve.tensor_tensor(mom[:, 3, :], mom[:, 1, :], mom[:, 1, :], ALU.mult))
                settle()
                done(dve.tensor_scalar(mom[:, 4, :], mom[:, 3, :], 0.25, EPS, ALU.mult, ALU.add))
                settle()
                dve.scalar_tensor_tensor(mom[:, 5, :], mom[:, 2, :], 1.0 / D, mom[:, 4, :],
                                         ALU.mult, ALU.add).then_inc(var_ready, 1)
                norms[0] += 1
                dve.wait_ge(std_ready, norms[0])
                done(dve.reciprocal(rstd[:, :], std[:, :]))
                settle()

            def normalise(dst, src, c):
                return dve.tensor_scalar(dst[:, c, :], src[:, c, :], mom[:, 0, c:c + 1], rstd[:, c:c + 1],
                                         ALU.subtract, ALU.mult)

            def norm_groups():
                moments(X)
                for c in range(C):
                    ins = normalise(tok_a, X, c)
                    if c % CQ == CQ - 1:
                        ins.then_inc(norm_ready, 1)

            def residual(f, last):
                moments(f)
                for c in range(C):
                    done(normalise(f, f, c))
                settle()
                for q in range(Q):
                    g = slice(q * CQ, (q + 1) * CQ)
                    ins = dve.tensor_tensor(X[:, g, :], X[:, g, :], f[:, g, :], ALU.add)
                    if last:
                        ins.then_inc(out_ready, 1)
                    else:
                        done(ins)
                settle()

            def ssm(l):
                norm_groups()
                half_v = dtT
                tiles = [(b, h) for b in range(BATCH) for h in range(H)]
                w_buf = yT
                dve.wait_ge(ld_ssm[l], 80)
                dve.wait_ge(a_exp_ready, l + 1)
                dve.tensor_scalar(a_sb[l][:, :, :], a_sb[l][:, :, :], -1.0, None, ALU.mult).then_inc(a_ready, 1)
                for h in range(H):
                    ins = dve.tensor_scalar(ddiag[:, h, :], ident[:, :], dskip_sb[l][:, h:h + 1], None, ALU.mult)
                ins.then_inc(ddiag_ready, 1)
                for i, (b, h) in enumerate(tiles):
                    t = slice(b * SEQ, (b + 1) * SEQ)
                    dve.wait_ge(exp_ready, 8 * l + i + 1)
                    dve.tensor_scalar(w_buf[:, h, t], uT[:, h, t], 1.0, None, ALU.add).then_inc(w_ready, 1)
                    dve.wait_ge(w_ready, 8 * l + i + 1)
                    dve.scalar_tensor_tensor(uT[:, h, t], w_buf[:, h, t], -1.0, uT[:, h, t], ALU.add,
                                             ALU.subtract).then_inc(err_ready, 1)
                for i, (b, h) in enumerate(tiles):
                    t = slice(b * SEQ, (b + 1) * SEQ)
                    dve.wait_ge(ln_ready, 8 * l + i + 1)
                    done(dve.scalar_tensor_tensor(dtT[:, h, t], dtT[:, h, t], 0.0, w_buf[:, h, t], ALU.max, ALU.add))
                    settle()
                    dve.tensor_tensor(dtT[:, h, t], dtT[:, h, t], uT[:, h, t], ALU.subtract).then_inc(dt_ready, 1)
                    dve.wait_ge(dt_ready, 8 * l + i + 1)
                    done(dve.tensor_tensor(uT[:, h, t], dtT[:, h, t], feat_a[:, h, t], ALU.mult))
                settle()
                base = l * BATCH * UNITS
                with dve.Fori(0, BATCH) as b:
                    for u in range(UNITS + 1):
                        n, h = u // H, u % H
                        if u < UNITS:
                            if h == 0:
                                dve.wait_ge(brep_ready, b * N + (l * BATCH * N + n + 1))
                            dve.wait_ge(state_free, b * UNITS + (base + u + 1))
                            dve.tensor_tensor(state[:, u % STATE_RING, :], uT[:, h, bass.ds(b * SEQ, SEQ)],
                                              brep[n % REP][:, :], ALU.mult).then_inc(b_ready, 1)
                        if u:
                            v = u - 1
                            dve.wait_ge(b_ready, b * UNITS + (base + u))
                            dve.wait_ge(abar_ready, b * UNITS + (base + u))
                            s = state[:, v % STATE_RING, :]
                            dve.tensor_tensor_scan(s, abar[:, v % ABAR_RING, :], s, 0.0, ALU.mult,
                                                   ALU.add).then_inc(h_ready, 1)
                dve.wait_ge(tr_copied, TR_AFTER_Y[l])
                residual(f_tok, False)

            TR_AFTER_Y = [16, 8 * 3 + 16]

            dve.wait_ge(ld_x, 16)
            dve.wait_ge(ld_const, 16)
            dve.tensor_copy(ident_bf[:, :], ident[:, :]).then_inc(fsign_in, 1)
            ssm(0)
            moments(X)
            for c in range(C):
                done(normalise(tok_a, X, c))
            settle()
            moments(tok_a)
            for c in range(C):
                done(normalise(tok_a, tok_a, c))
            settle()
            dve.wait_ge(ld_ffn, 80)
            for q in range(Q):
                g = slice(q * CQ, (q + 1) * CQ)
                gb = gamma_sb[:, :].unsqueeze(1).to_broadcast([P, CQ, D])
                bb = beta_sb[:, :].unsqueeze(1).to_broadcast([P, CQ, D])
                done(dve.tensor_tensor(tok_a[:, g, :], tok_a[:, g, :], gb, ALU.mult))
                settle()
                dve.tensor_tensor(tok_a[:, g, :], tok_a[:, g, :], bb, ALU.add).then_inc(xsign_in, 1)
            for h in range(H):
                done(dve.bn_stats(st6[:, h, :], fw_sb[:, h, :]))
            settle()
            done(dve.tensor_tensor(mom[:, 0, 0:H], st6[:, 0:H, 1], st6[:, 0:H, 4], ALU.add))
            settle()
            done(dve.tensor_scalar(mom[:, 0, 0:H], mom[:, 0, 0:H], 0.5, None, ALU.mult))
            settle()
            for h in range(H):
                ins = dve.tensor_scalar(fw_sb[:, h, :], fw_sb[:, h, :], mom[:, 0, h:h + 1], None, ALU.subtract)
            ins.then_inc(fsign_in, 1)
            for c in range(C):
                dve.wait_ge(ffn_ready, c + 1)
                dve.tensor_tensor(f_tok[:, c, :], work[c % 2][:, 0:D], bias_sb[:, :], ALU.add).then_inc(ffn_used, 1)
                dve.wait_ge(ffn_used, c + 1)
                done(dve.tensor_tensor(f_tok[:, c, :], f_tok[:, c, :], alpha_sb[:, :], ALU.mult))
            settle()
            residual(f_tok, False)
            ssm(1)
            norm_groups()
            dve.wait_ge(ld_gate, 32)
            dve.wait_ge(gate_ready, 1)
            logits = work[0][:, 0:C * E].rearrange("p (c e) -> p c e", c=C)
            done(dve.tensor_reduce(psum_e[:, :], logits, AX.X, ALU.max))
            settle()
            dve.tensor_tensor(probs[:, :, :], logits, psum_e[:, :].unsqueeze(2).to_broadcast([P, C, E]),
                              ALU.subtract).then_inc(sm_in, 1)
            dve.wait_ge(sm_out, 1)
            done(dve.tensor_reduce(psum_e[:, :], probs[:, :, :], AX.X, ALU.add))
            settle()
            done(dve.reciprocal(psum_e[:, :], psum_e[:, :]))
            settle()
            done(dve.tensor_tensor(probs[:, :, :], probs[:, :, :], psum_e[:, :].unsqueeze(2).to_broadcast([P, C, E]),
                                   ALU.mult))
            settle()
            for c in range(C):
                done(dve.max(top8[:, c, :], probs[:, c, :]))
            settle()
            for c in range(C):
                done(dve.max_index(top8i[:, c, :], top8[:, c, :], probs[:, c, :]))
            settle()
            done(dve.tensor_copy(top8f[:, :, :], top8i[:, :, 0:2]))
            done(dve.memset(wsel[:, :, E:ES], 1.0))
            settle()
            for c in range(C):
                done(dve.tensor_scalar(wsel[:, c, 0:E], iota_sb[:, :], top8f[:, c, 0:1], top8[:, c, 0:1],
                                       ALU.is_equal, ALU.mult))
                done(dve.tensor_scalar(wsel2[:, c, :], iota_sb[:, :], top8f[:, c, 1:2], top8[:, c, 1:2],
                                       ALU.is_equal, ALU.mult))
            settle()
            done(dve.tensor_tensor(wsel[:, :, 0:E], wsel[:, :, 0:E], wsel2[:, :, :], ALU.add))
            settle()

            for c in range(C):
                def step(e, slot, at):
                    dve.wait_ge(silu_ready, at + 1)
                    dve.scalar_tensor_tensor(gated[:, slot, :], silu[:, slot, :], wsel[:, c, bass.ds(e, 1)],
                                             bank[slot][:, INTER:2 * INTER], ALU.mult, ALU.mult).then_inc(gated_ready, 1)
                    dve.wait_ge(gT_ready, at + 1)
                    dve.tensor_copy(gatedT[0:IR, slot, 1, :], work[slot][0:IR, 0:P]).then_inc(gTb_copied, 1)
                with dve.Fori(0, ES - 1, 2) as e:
                    step(e, 0, e + c * ES)
                    step(e + 1, 1, e + (c * ES + 1))
            dve.wait_ge(moe_copied, C)
            residual(tok_a, True)

        @block.scalar
        def _(act):
            roots = [0]
            groups = [0]

            def root():
                roots[0] += 1
                act.wait_ge(var_ready, roots[0])
                act.activation(std[:, :], mom[:, 5, :], ACT.Sqrt).then_inc(std_ready, 1)

            def copy_groups(dst):
                for q in range(Q):
                    for h in range(H):
                        i = groups[0]
                        act.wait_ge(tr_ready, i + 1)
                        act.activation(dst(q, h), work[i % 2][:, :], ACT.Copy).then_inc(tr_copied, 1)
                        groups[0] += 1

            def feature_major(q, h):
                return feat_a[:, h, q * CQ * P:(q + 1) * CQ * P]

            def ssm(l):
                act.wait_ge(ld_ssm[l], 80)
                act.activation(a_sb[l][:, :, :], a_sb[l][:, :, :], ACT.Exp).then_inc(a_exp_ready, 1)
                root()
                copy_groups(feature_major)
                for b in range(BATCH):
                    t = slice(b * SEQ, (b + 1) * SEQ)
                    act.wait_ge(proj_ready, 8 * l + 2 * b + 1)
                    act.activation(dtpT[0:RANK[l], t], ysum[0][0:RANK[l], :], ACT.Copy).then_inc(proj_copied, 1)
                    act.wait_ge(proj_ready, 8 * l + 2 * b + 2)
                    act.activation(bcT[:, t], ysum[1][0:2 * N, :], ACT.Copy).then_inc(proj_copied, 1)
                tiles = [(b, h) for b in range(BATCH) for h in range(H)]
                for i, (b, h) in enumerate(tiles):
                    t = slice(b * SEQ, (b + 1) * SEQ)
                    act.wait_ge(pre_ready, 8 * l + i + 1)
                    act.activation(dtT[:, h, t], work[i % 2][:, :], ACT.Identity, bias=bdt_sb[l][:, h:h + 1])
                    act.activation(uT[:, h, t], work[i % 2][:, :], ACT.Abs, bias=bdt_sb[l][:, h:h + 1])\
                       .then_inc(pre_used, 1)
                    act.wait_ge(pre_used, 8 * l + i + 1)
                    act.activation(uT[:, h, t], uT[:, h, t], ACT.Exp, scale=-1.0).then_inc(exp_ready, 1)
                for i, (b, h) in enumerate(tiles):
                    t = slice(b * SEQ, (b + 1) * SEQ)
                    act.wait_ge(err_ready, 8 * l + i + 1)
                    act.activation(yT[:, h, t], yT[:, h, t], ACT.Ln).then_inc(ln_ready, 1)
                act.wait_ge(a_ready, l + 1)
                act.wait_ge(dt_ready, 8 * (l + 1))
                base = l * BATCH * UNITS
                nbase = l * BATCH * N
                with act.Fori(0, BATCH) as b:
                    for n in range(N):
                        if n * H >= ABAR_RING:
                            act.wait_ge(h_ready, b * UNITS + (base + (n + 1) * H - ABAR_RING))
                        act.wait_ge(crep_ready, b * N + (nbase + n + 1))
                        if n >= CREP_RING:
                            act.wait_ge(hc_ready, b * UNITS + (base + H * (n - CREP_RING + 1)))
                        act.activation(crep[:, n % CREP_RING, :], cps[n % REP][:, :], ACT.Copy)\
                           .then_inc(crep_copied, 1)
                        for h in range(H):
                            u = n * H + h
                            act.activation(abar[:, u % ABAR_RING, :], dtT[:, h, bass.ds(b * SEQ, SEQ)], ACT.Exp,
                                           scale=a_sb[l][:, h, n:n + 1]).then_inc(abar_ready, 1)
                    act.wait_ge(state_free, b * UNITS + (base + UNITS + STATE_RING))
                    act.nop()
                    for h in range(H):
                        act.activation(yT[:, h, bass.ds(b * SEQ, SEQ)], ysum[h][:, :], ACT.Copy)\
                           .then_inc(ysum_free, 1)
                for q in range(Q):
                    for h in range(H):
                        i = groups[0]
                        act.wait_ge(tr_ready, i + 1)
                        act.activation(f_tok[:, q * CQ + 2 * h:q * CQ + 2 * h + 2, :],
                                       work[i % 2][:, :].rearrange("p (c d) -> p c d", c=2), ACT.Copy)\
                           .then_inc(tr_copied, 1)
                        groups[0] += 1
                root()

            ssm(0)
            root()
            root()
            for q in range(Q):
                g = slice(q * CQ, (q + 1) * CQ)
                act.wait_ge(xsign_in, q + 1)
                act.activation(a_sign[:, g, :], tok_a[:, g, :], ACT.Sign).then_inc(xsign_out, 1)
            act.wait_ge(fsign_in, 2)
            act.activation(fw_sign[:, :, :], fw_sb[:, :, :], ACT.Sign).then_inc(fsign_out, 1)
            act.wait_ge(fwT_ready, 1)
            act.activation(fw_signT[:, :, :], work[0][:, 0:D].bitcast(BF16).rearrange("p (h d) -> p h d", h=H),
                           ACT.Copy).then_inc(fwT_copied, 1)
            for q in range(Q):
                for h in range(H):
                    i = groups[0]
                    act.wait_ge(tr_ready, i + 1)
                    act.activation(a_signT[:, h, q * CQ * P:(q + 1) * CQ * P],
                                   work[i % 2][:, 0:CQ * P // 2].bitcast(BF16), ACT.Copy).then_inc(tr_copied, 1)
                    groups[0] += 1
            root()
            ssm(1)
            root()
            copy_groups(feature_major)
            act.wait_ge(sm_in, 1)
            act.activation(probs[:, :, :], probs[:, :, :], ACT.Exp).then_inc(sm_out, 1)
            for c in range(C):
                def step(slot, at):
                    act.wait_ge(up_ready, at + 1)
                    act.activation(silu[:, slot, :], bank[slot][:, 0:INTER], ACT.Silu).then_inc(silu_ready, 1)
                    act.wait_ge(gT_ready, at + 1)
                    act.activation(gatedT[:, slot, 0, :], bank[2 + slot][:, 0:P], ACT.Copy).then_inc(gTa_copied, 1)
                with act.Fori(0, ES - 1, 2) as e:
                    step(0, e + c * ES)
                    step(1, e + (c * ES + 1))
                act.wait_ge(moe_ready, c + 1)
                act.activation(tok_a[:, c, :], ysum[c % 2][:, 0:D], ACT.Copy).then_inc(moe_copied, 1)
            root()

        @block.gpsimd
        def _(pool):
            for l in range(2):
                base, nbase = l * BATCH * UNITS, l * BATCH * N
                with pool.Fori(0, BATCH) as b:
                    for u in range(UNITS):
                        n, h = u // H, u % H
                        if h == 0:
                            pool.wait_ge(crep_copied, b * N + (nbase + n + 1))
                        pool.wait_ge(h_ready, b * UNITS + (base + u + 1))
                        s = state[:, u % STATE_RING, :]
                        pool.tensor_tensor(s, s, crep[:, n % CREP_RING, :], ALU.mult).then_inc(hc_ready, 1)

        @block.tensor
        def _(pe):
            groups = [0]
            normed = [0]

            def transposes(src, eye_sb, width):
                for q in range(Q):
                    yield q
                    for h in range(H):
                        i = groups[0]
                        if i >= 2:
                            pe.wait_ge(tr_copied, i - 1)
                        o = work[i % 2]
                        o = o[:, 0:CQ * P // 2].bitcast(BF16) if width == 2 else o[:, :]
                        for k in range(CQ):
                            ins = pe.transpose(o[:, k * P:(k + 1) * P], src[:, q * CQ + k, h * P:(h + 1) * P], eye_sb[:, :])
                        ins.then_inc(tr_ready, 1)
                        groups[0] += 1

            def norm_transposes():
                for q in transposes(tok_a, ident, 4):
                    pe.wait_ge(norm_ready, normed[0] + q + 1)
                normed[0] += Q

            def ssm(l):
                pe.wait_ge(ld_const, 16)
                norm_transposes()
                r = RANK[l]
                pe.wait_ge(ld_ssm[l], 80)
                for b in range(BATCH):
                    t = slice(b * SEQ, (b + 1) * SEQ)
                    pe.wait_ge(tr_copied, groups[0] - 2 * (Q - 1 - b))
                    if b or l:
                        pe.wait_ge(proj_copied, 8 * l + 2 * b)
                    if l:
                        pe.wait_ge(ysum_free, H + H * BATCH)
                    for h in range(H):
                        ins = pe.matmul(ysum[0][0:r, :], win_sb[l][:, h, 0:r], feat_a[:, h, t], start=h == 0, stop=h == H - 1)
                    ins.then_inc(proj_ready, 1)
                    for h in range(H):
                        ins = pe.matmul(ysum[1][0:2 * N, :], win_sb[l][:, h, r:r + 2 * N], feat_a[:, h, t],
                                        start=h == 0, stop=h == H - 1)
                    ins.then_inc(proj_ready, 1)
                for b in range(BATCH):
                    t = slice(b * SEQ, (b + 1) * SEQ)
                    pe.wait_ge(proj_copied, 8 * l + 2 * b + 1)
                    for h in range(H):
                        i = 8 * l + 2 * b + h
                        if i % 8 >= 2:
                            pe.wait_ge(pre_used, i - 1)
                        pe.matmul(work[i % 2][:, :], wdt_sb[l][:, h * P:(h + 1) * P], dtpT[0:r, t],
                                  start=True, stop=True).then_inc(pre_ready, 1)
                base, nbase = l * BATCH * UNITS, l * BATCH * N
                pe.wait_ge(proj_copied, 8 * (l + 1))
                pe.wait_ge(ddiag_ready, l + 1)
                pe.wait_ge(pre_used, 8 * (l + 1))

                def replicate(b, n):
                    rhs = bcT[:, bass.ds(b * SEQ, SEQ)]
                    pe.matmul(brep[n % REP][:, :], ident[0:2 * N, n:n + 1].to_broadcast([2 * N, P]), rhs,
                              start=True, stop=True).then_inc(brep_ready, 1)
                    pe.matmul(cps[n % REP][:, :], ident[0:2 * N, N + n:N + n + 1].to_broadcast([2 * N, P]), rhs,
                              start=True, stop=True).then_inc(crep_ready, 1)

                with pe.Fori(0, BATCH) as b:
                    for n in range(REP):
                        replicate(b, n)
                    for h in range(H):
                        pe.wait_ge(ysum_free, b * H + (l * BATCH * H + h + 1))
                        pe.matmul(ysum[h][:, :], ddiag[:, h, :], feat_a[:, h, bass.ds(b * SEQ, SEQ)], start=True, stop=False)
                    for n in range(N):
                        for h in range(H):
                            u = n * H + h
                            pe.wait_ge(hc_ready, b * UNITS + (base + u + 1))
                            pe.matmul(ysum[h][:, :], ident[:, :], state[:, u % STATE_RING, :], start=False,
                                      stop=n == N - 1).then_inc(state_free, 1)
                        if n + REP < N:
                            replicate(b, n + REP)
                for q in range(Q):
                    pe.wait_ge(ysum_free, H + (l * BATCH + q + 1) * H)
                    for j in range(2):
                        i = groups[0]
                        pe.wait_ge(tr_copied, i - 1)
                        for k in range(2):
                            c = q * CQ + 2 * j + k
                            for h in range(H):
                                ins = pe.transpose(work[i % 2][:, (k * H + h) * P:(k * H + h + 1) * P],
                                                   yT[:, h, c * P:(c + 1) * P], ident[:, :])
                        ins.then_inc(tr_ready, 1)
                        groups[0] += 1

            pe.sem_inc(state_free, STATE_RING)
            pe.sem_inc(ysum_free, H)
            ssm(0)
            pe.wait_ge(fsign_out, 1)
            pe.wait_ge(tr_copied, groups[0])
            for k in range(H):
                for h in range(H):
                    o = work[0][:, 0:D].bitcast(BF16)[:, k * D + h * P:k * D + (h + 1) * P]
                    ins = pe.transpose(o, fw_sign[:, h, k * P:(k + 1) * P], ident_bf[:, :])
            ins.then_inc(fwT_ready, 1)
            pe.wait_ge(fwT_copied, 1)
            for q in transposes(a_sign, ident_bf, 2):
                pe.wait_ge(xsign_out, q + 1)
            pe.wait_ge(tr_copied, groups[0])
            for c in range(C):
                if c >= 2:
                    pe.wait_ge(ffn_used, c - 1)
                for h in range(H):
                    ins = pe.matmul(work[c % 2][:, 0:D], a_signT[:, h, c * P:(c + 1) * P], fw_signT[:, h, :],
                                    start=h == 0, stop=h == H - 1)
                ins.then_inc(ffn_ready, 1)
            pe.wait_ge(ffn_used, C)
            ssm(1)
            norm_transposes()
            pe.wait_ge(tr_copied, groups[0])
            pe.wait_ge(ld_gate, 32)
            for c in range(C):
                for h in range(H):
                    ins = pe.matmul(work[0][:, c * E:(c + 1) * E], feat_a[:, h, c * P:(c + 1) * P], gatew_sb[:, h, :],
                                    start=h == 0, stop=h == H - 1)
            ins.then_inc(gate_ready, 1)
            pe.wait_ge(ld_w13, 16 * H)
            pe.wait_ge(ld_w2, 32)

            def up(c, e, slot, at, wait):
                if wait:
                    pe.wait_ge(gated_ready, at - 1)
                for h in range(H):
                    ins = pe.matmul(bank[slot][:, 0:2 * INTER], feat_a[:, h, c * P:(c + 1) * P], w13_sb[:, h, e, :],
                                    start=h == 0, stop=h == H - 1)
                ins.then_inc(up_ready, 1)

            def turn(slot, at):
                pe.wait_ge(gated_ready, at + 1)
                pe.transpose(bank[2 + slot][:, 0:P], gated[:, slot, 0:P], ident[:, :])
                pe.transpose(work[slot][0:IR, 0:P], gated[:, slot, P:INTER], ident[:, :]).then_inc(gT_ready, 1)

            def down(c, e, slot, at, first, last):
                pe.wait_ge(gTa_copied, at + 1)
                pe.matmul(ysum[c % 2][:, 0:D], gatedT[:, slot, 0, :], w2a[:, e, :], start=first, stop=False)
                pe.wait_ge(gTb_copied, at + 1)
                ins = pe.matmul(ysum[c % 2][:, 0:D], gatedT[0:IR, slot, 1, :], w2b[:, e, :], start=False, stop=last)
                if last:
                    ins.then_inc(moe_ready, 1)

            for c in range(C):
                at = c * ES
                if c >= 2:
                    pe.wait_ge(moe_copied, c - 1)
                up(c, 0, 0, at, c > 0)
                up(c, 1, 1, at + 1, c > 0)
                turn(0, at)
                up(c, 2, 0, at + 2, True)
                turn(1, at + 1)
                down(c, 0, 0, at, True, False)
                with pe.Fori(3, ES - 1, 2) as e:
                    for j in range(2):
                        up(c, e + j if j else e, (1 + j) % 2, e + (at + j), True)
                        turn(j, e + (at + j - 1))
                        down(c, e + (j - 2), (1 + j) % 2, e + (at + j - 2), False, False)
                up(c, ES - 1, 1, at + ES - 1, True)
                turn(0, at + ES - 2)
                down(c, ES - 3, 1, at + ES - 3, False, False)
                turn(1, at + ES - 1)
                down(c, ES - 2, 0, at + ES - 2, False, False)
                down(c, ES - 1, 1, at + ES - 1, False, True)


def kernel(**inputs):
    import numpy as np
    import concourse.bacc as bacc
    from concourse import mybir as mb
    from concourse.bass_utils import run_bass_kernel_spmd as launch

    i = {k: np.asarray(v) for k, v in inputs.items()}
    sw1, sw3 = (i[f"L1_ffn_{n}"].reshape(ES - E, INTER, D) for n in ("sw1", "sw3"))
    sw2 = i["L1_ffn_sw2"].reshape(D, ES - E, INTER).transpose(1, 0, 2)
    w1, w3, w2 = (np.concatenate([i[f"L1_ffn_{n}"], s]) for n, s in (("w1", sw1), ("w3", sw3), ("w2", sw2)))
    arrays = {
        "x": i["L0_attn_x"].reshape(T, D),
        "eye": np.eye(P, dtype=np.float32),
        "a_log0": i["L0_attn_A_log"], "a_log1": i["L1_attn_A_log"],
        "d_skip0": i["L0_attn_D"].reshape(H, P).T, "d_skip1": i["L1_attn_D"].reshape(H, P).T,
        "w_in0": i["L0_attn_W_xproj"].T,
        "w_in1": np.concatenate([i["L1_attn_W_delta"], i["L1_attn_W_B"], i["L1_attn_W_C"]], axis=1),
        "w_dt0": i["L0_attn_W_dt"].T, "w_dt1": i["L1_attn_W_dt"],
        "b_dt0": i["L0_attn_b_dt"].reshape(H, P).T, "b_dt1": i["L1_attn_b_dt"].reshape(H, P).T,
        "gamma": i["L0_ffn_gamma"], "beta": i["L0_ffn_beta"], "weight": i["L0_ffn_weight"],
        "bias": i["L0_ffn_bias"], "alpha": i["L0_ffn_alpha"],
        "gate_wt": i["L1_ffn_gate_w"].T, "iota_e": np.arange(E, dtype=np.float32),
        "w13": np.concatenate([w1, w3], axis=1).transpose(0, 2, 1), "w2": w2.transpose(0, 2, 1),
    }
    arrays = {k: np.ascontiguousarray(v) for k, v in arrays.items()}
    nc = bacc.Bacc("TRN2", target_bir_lowering=False, num_devices=1)
    ap = {k: nc.dram_tensor(k, v.shape, mb.dt.from_np(v.dtype), kind="ExternalInput").ap() for k, v in arrays.items()}
    for k in ("a_log", "d_skip", "w_in", "w_dt", "b_dt"):
        ap[k] = [ap.pop(f"{k}{l}") for l in range(2)]
    ap["out"] = nc.dram_tensor("out", (T, D), F32, kind="ExternalOutput").ap()
    sandwich_kernel(nc, **ap)
    r = launch(nc, [arrays], core_ids=[0])
    return r.results[0]["out"].reshape(BATCH, SEQ, D)
```

```python
import concourse.bass as bass
from concourse import mybir
from contextlib import ExitStack

F32 = mybir.dt.float32
BF16 = mybir.dt.bfloat16
U32 = mybir.dt.uint32
ALU = mybir.AluOpType
ACT = mybir.ActivationFunctionType
AX = mybir.AxisListType

P = 128
D = 256
H = D // P
BATCH, SEQ = 4, 512
T = BATCH * SEQ
C = T // P
CQ = 4
Q = C // CQ
N = 16
RANK = (64, 128)
E = 16
ES = 18
INTER = 176
IR = INTER - P
EPS = 1e-5
UNITS = N * H
STATE_RING, ABAR_RING, CREP_RING = 8, 4, 4
TILES = 2 * T // P + E
LOADS = 4
REP = 3


def sandwich_kernel(nc, x, eye, spread, a_log, d_skip, w_in, w_dt, b_dt, gamma, beta, weight, bias, alpha,
                    gate_wt, upper, counts, w13, w2, x_sorted, y_sorted, out):
    ctx = ExitStack()
    with ctx:
        def sb(name, shape, dt=F32):
            return ctx.enter_context(nc.sbuf_tensor(name, shape, dt))

        def sem(name):
            return ctx.enter_context(nc.semaphore(name))

        X = sb("residual", [P, C, D])
        tok_a = sb("tok_a", [P, C, D])
        feat_a = sb("feat_a", [P, H, T])
        arena = sb("arena", [P, 3 * H * T // 1])
        dtT = arena[:, 0:H * T].rearrange("p (h t) -> p h t", h=H)
        uT = arena[:, H * T:2 * H * T].rearrange("p (h t) -> p h t", h=H)
        state = arena[:, 2 * H * T:2 * H * T + STATE_RING * SEQ].rearrange("p (r t) -> p r t", r=STATE_RING)
        w2a = arena[:, 0:ES * D].rearrange("p (e d) -> p e d", e=ES)
        w2b = arena[0:IR, ES * D:2 * ES * D].rearrange("p (e d) -> p e d", e=ES)
        yT = tok_a[:, :, :].rearrange("p c d -> p (c d)").rearrange("p (h t) -> p h t", h=H)
        f_tok = feat_a[:, :, :].rearrange("p h t -> p (h t)").rearrange("p (c d) -> p c d", c=C)
        rings = sb("rings", [P, (ABAR_RING + CREP_RING) * SEQ + 2 * T])
        ring_end = (ABAR_RING + CREP_RING) * SEQ
        abar = rings[:, 0:ABAR_RING * SEQ].rearrange("p (r t) -> p r t", r=ABAR_RING)
        crep = rings[:, ABAR_RING * SEQ:ring_end].rearrange("p (r t) -> p r t", r=CREP_RING)
        bcT = rings[:, ring_end:ring_end + T // 2].bitcast(BF16)
        dtpT = rings[:, ring_end + T:ring_end + 2 * T]
        f_moe = rings[:, 0:C * D].rearrange("p (c d) -> p c d", c=C)
        tile_x = rings[:, C * D:C * D + LOADS * D].rearrange("p (r d) -> p r d", r=LOADS)
        tile_y = rings[:, C * D + LOADS * D:C * D + 2 * LOADS * D].rearrange("p (r d) -> p r d", r=LOADS)
        tile_xT = rings[:, C * D + 2 * LOADS * D:C * D + (2 * LOADS + 2) * D]\
            .rearrange("p (r h t) -> p r h t", r=2, h=H)
        w13_sb = sb("w13_sb", [P, H, ES, 2 * INTER])
        ident = sb("ident", [P, P])
        spread_f = sb("spread_f", [P, 2 * N])
        spread_bf = sb("spread_bf", [P, 2 * N], BF16)
        bcw_sb = [sb(f"bcw_sb{l}", [P, H, 4, 2 * N]) for l in range(2)]
        ident_bf = sb("ident_bf", [P, P], BF16)
        a_sb = [sb(f"a_sb{l}", [P, H, N]) for l in range(2)]
        dskip_sb = [sb(f"dskip_sb{l}", [P, H]) for l in range(2)]
        ddiag = sb("ddiag", [P, H, P])
        win_sb = [sb(f"win_sb{l}", [P, H, RANK[l] + 2 * N]) for l in range(2)]
        wdt_sb = [sb(f"wdt_sb{l}", [RANK[l], D]) for l in range(2)]
        bdt_sb = [sb(f"bdt_sb{l}", [P, H]) for l in range(2)]
        gamma_sb, beta_sb, bias_sb, alpha_sb = (sb(f"{n}_sb", [P, D]) for n in ("gamma", "beta", "bias", "alpha"))
        fw_sb = sb("fw_sb", [P, H, D])
        fw_sign = sb("fw_sign", [P, H, D], BF16)
        fw_signT = sb("fw_signT", [P, H, D], BF16)
        gatew_sb = sb("gatew_sb", [P, H, E])
        upper_sb = sb("upper_sb", [P, P])
        ones = sb("ones", [P, P])
        zeros = sb("zeros", [P, D])
        counts_sb = sb("counts_sb", [P, 2 * E + TILES + E * C])
        iota_e = counts_sb[:, 0:E]
        iota_rows = counts_sb[:, E:2 * E]
        iota_tile = counts_sb[:, 2 * E:2 * E + TILES]
        not_first = counts_sb[:, 2 * E + TILES:]
        route = arena[:, 2 * ES * D:]
        cut = [0]

        def part(*shape):
            size = 1
            for n in shape:
                size *= n
            view = route[:, cut[0]:cut[0] + size]
            cut[0] += size
            return view.rearrange("p (a b) -> p a b", a=shape[0])

        onehot = [part(C, E), part(C, E)]
        picked = part(C, E)
        chunk_count, chunk_end = part(E, C), part(E, C)
        more_rows = part(E, E)
        past_end = part(TILES, E)
        slot = part(C, E)
        slot_k = part(C, E)
        tiles_e, tile_end, row0 = (sb(n, [P, E]) for n in ("tiles_e", "tile_end", "row0"))
        slot_f = sb("slot_f", [P, 2, C])
        slot_u = [sb(f"slot_u{k}", [P, C], U32) for k in range(2)]
        tile_ef = sb("tile_ef", [P, TILES])
        tile_e = sb("tile_e", [P, TILES], U32)
        y_k = [tok_a, w13_sb[:, 0].rearrange("p e i -> p (e i)")[:, 0:C * D].rearrange("p (c d) -> p c d", c=C)]
        st6 = sb("st6", [P, C, 6])
        mom = sb("mom", [P, 6, C])
        std = sb("std", [P, C])
        rstd = sb("rstd", [P, C])
        probs = sb("probs", [P, C, E])
        psum_e = sb("psum_e", [P, C])
        top8 = sb("top8", [P, C, 8])
        top8i = sb("top8i", [P, C, 8], U32)
        top8f = sb("top8f", [P, C, 2])
        silu = sb("silu", [P, 2, INTER])
        gated = sb("gated", [P, 2, INTER])
        gatedT = sb("gatedT", [P, 2, 2, P])
        a_sign = arena[:, 0:H * T // 2].bitcast(BF16).rearrange("p (c d) -> p c d", c=C)
        a_signT = arena[:, H * T // 2:H * T].bitcast(BF16).rearrange("p (h t) -> p h t", h=H)

        bank = [ctx.enter_context(nc.psum_tensor(f"bank{i}", [P, 512], F32)) for i in range(8)]
        brep = [bank[0], bank[1], bank[6]]
        cps = [bank[2], bank[3], bank[7]]
        ysum = bank[4:6]
        work = bank[6:8]

        ld_x, ld_const, ld_ffn, ld_gate, ld_w13, ld_w2, stored = (
            sem(n) for n in ("ld_x", "ld_const", "ld_ffn", "ld_gate", "ld_w13", "ld_w2", "stored"))
        ld_ssm = [sem(f"ld_ssm{l}") for l in range(2)]
        dve_done = sem("dve_done")
        var_ready, std_ready = sem("var_ready"), sem("std_ready")
        norm_ready = sem("norm_ready")
        tr_ready, tr_copied = sem("tr_ready"), sem("tr_copied")
        proj_ready, proj_copied = sem("proj_ready"), sem("proj_copied")
        pre_ready, pre_used = sem("pre_ready"), sem("pre_used")
        exp_ready, w_ready, err_ready, ln_ready = (
            sem(n) for n in ("exp_ready", "w_ready", "err_ready", "ln_ready"))
        dt_ready = sem("dt_ready")
        a_exp_ready, a_ready, ddiag_ready = sem("a_exp_ready"), sem("a_ready"), sem("ddiag_ready")
        bcw_ready, bc_high, bc_rest, bc_mid, bc_ready = (
            sem(n) for n in ("bcw_ready", "bc_high", "bc_rest", "bc_mid", "bc_ready"))
        brep_ready, crep_ready, crep_copied = sem("brep_ready"), sem("crep_ready"), sem("crep_copied")
        abar_ready, b_ready, h_ready, hc_ready = (
            sem(n) for n in ("abar_ready", "b_ready", "h_ready", "hc_ready"))
        state_free = sem("state_free")
        ysum_free = sem("ysum_free")
        fsign_in, fsign_out, fwT_ready, fwT_copied = (
            sem(n) for n in ("fsign_in", "fsign_out", "fwT_ready", "fwT_copied"))
        xsign_in, xsign_out = sem("xsign_in"), sem("xsign_out")
        ffn_ready, ffn_used = sem("ffn_ready"), sem("ffn_used")
        gate_ready, sm_in, sm_out = sem("gate_ready"), sem("sm_in"), sem("sm_out")
        up_ready, silu_ready, gated_ready, gT_ready, gT_copied, moe_ready, moe_copied = (
            sem(n) for n in ("up_ready", "silu_ready", "gated_ready", "gT_ready", "gT_copied", "moe_ready", "moe_copied"))
        onehot_ready, prefix_ready, slots_ready, experts_ready = (
            sem(n) for n in ("onehot_ready", "prefix_ready", "slots_ready", "experts_ready"))
        zeros_ready, sorted_zeroed, sorted_ready = sem("zeros_ready"), sem("sorted_zeroed"), sem("sorted_ready")
        x_loaded = [sem(f"x_loaded{k}") for k in range(LOADS)]
        y_stored = [sem(f"y_stored{k}") for k in range(LOADS)]
        xt_ready, xt_copied, tup_ready, tsilu_ready, tgated_ready, tgT_ready, tgT_copied, ty_ready, ty_copied = (
            sem(n) for n in ("xt_ready", "xt_copied", "tup_ready", "tsilu_ready", "tgated_ready", "tgT_ready",
                             "tgT_copied", "ty_ready", "ty_copied"))
        y_gathered = [sem(f"y_gathered{k}") for k in range(2)]
        out_ready = sem("out_ready")

        block = ctx.enter_context(nc.Block())

        @block.sync
        def _(sp):
            sp.dma_start(X[:, :, :], x.rearrange("(c p) d -> p c d", p=P)).then_inc(ld_x, 16)
            sp.dma_start(ident[:, :], eye).then_inc(ld_const, 16)
            sp.dma_start(spread_f[:, :], spread).then_inc(ld_const, 16)
            for l in range(2):
                for dst, src in ((a_sb[l], a_log[l]), (dskip_sb[l], d_skip[l]), (bdt_sb[l], b_dt[l])):
                    view = src.rearrange("(h p) n -> p h n", p=P) if dst is a_sb[l] else src
                    sp.dma_start(dst[:], view).then_inc(ld_ssm[l], 16)
                sp.dma_start(win_sb[l][:, :, :], w_in[l].rearrange("(h p) r -> p h r", p=P)).then_inc(ld_ssm[l], 16)
                sp.dma_start(wdt_sb[l][:, :], w_dt[l]).then_inc(ld_ssm[l], 16)
            sp.dma_start(fw_sb[:, :, :], weight.rearrange("(h p) d -> p h d", p=P)).then_inc(ld_ffn, 16)
            for dst, src in ((gamma_sb, gamma), (beta_sb, beta), (bias_sb, bias), (alpha_sb, alpha)):
                sp.dma_start(dst[:, :], src.partition_broadcast(P)).then_inc(ld_ffn, 16)
            sp.dma_start(gatew_sb[:, :, :], gate_wt.rearrange("(h p) e -> p h e", p=P)).then_inc(ld_gate, 16)
            sp.dma_start(upper_sb[:, :], upper).then_inc(ld_gate, 16)
            sp.dma_start(counts_sb[:, :], counts.partition_broadcast(P)).then_inc(ld_gate, 16)
            for h in range(H):
                sp.dma_start(w13_sb[:, h], w13[:, h * P:(h + 1) * P, :].rearrange("e p i -> p e i")).then_inc(ld_w13, 16)
            sp.wait_ge(ysum_free, H + 2 * BATCH * H)
            sp.dma_start(w2a, w2[:, 0:P, :].rearrange("e p d -> p e d")).then_inc(ld_w2, 16)
            sp.dma_start(w2b, w2[:, P:INTER, :].rearrange("e p d -> p e d")).then_inc(ld_w2, 16)
            sp.wait_ge(zeros_ready, 1)
            sp.dma_start(x_sorted.rearrange("(t p) d -> p t d", p=P),
                         zeros[:, :].unsqueeze(1).to_broadcast([P, TILES, D])).then_inc(sorted_zeroed, 16)
            x_tiles = x_sorted.rearrange("(t p) d -> t p d", p=P)
            y_tiles = y_sorted.rearrange("(t p) d -> t p d", p=P)
            sp.wait_ge(sorted_ready, 16 * 2 * C)
            for k in range(LOADS):
                sp.dma_start(tile_x[:, k, :], x_tiles[k]).then_inc(x_loaded[k], 16)
            with sp.Fori(0, TILES // LOADS - 1) as m:
                for k in range(LOADS):
                    sp.wait_ge(xt_ready, m * LOADS + (k + 1))
                    sp.dma_start(tile_x[:, k, :], x_tiles[bass.ds(m * LOADS + (k + LOADS), 1)].rearrange("t p d -> (t p) d"))\
                      .then_inc(x_loaded[k], 16)
                    sp.wait_ge(ty_copied, m * LOADS + (k + 1))
                    sp.dma_start(y_tiles[bass.ds(m * LOADS + k, 1)].rearrange("t p d -> (t p) d"), tile_y[:, k, :])\
                      .then_inc(y_stored[k], 16)
            for k in range(LOADS):
                sp.wait_ge(ty_copied, TILES - LOADS + k + 1)
                sp.dma_start(y_tiles[TILES - LOADS + k], tile_y[:, k, :]).then_inc(y_stored[k], 16)
            for q in range(Q):
                sp.wait_ge(out_ready, q + 1)
                sp.dma_start(out.rearrange("(c p) d -> p c d", p=P)[:, q * CQ:(q + 1) * CQ, :],
                             X[:, q * CQ:(q + 1) * CQ, :]).then_inc(stored, 16)
            sp.wait_ge(stored, 16 * Q)

        @block.vector
        def _(dve):
            steps = [0]
            norms = [0]

            def done(ins, times=1):
                steps[0] += times
                return ins.then_inc(dve_done, 1)

            def settle():
                dve.wait_ge(dve_done, steps[0])

            def moments(src):
                with dve.Fori(0, C) as c:
                    done(dve.bn_stats(st6[:, bass.ds(c, 1), :], src[:, bass.ds(c, 1), :]), 0)
                steps[0] += C
                settle()
                s = st6[:, :, :]
                done(dve.tensor_tensor(mom[:, 0, :], s[:, :, 1], s[:, :, 4], ALU.add))
                done(dve.tensor_tensor(mom[:, 1, :], s[:, :, 1], s[:, :, 4], ALU.subtract))
                done(dve.tensor_tensor(mom[:, 2, :], s[:, :, 2], s[:, :, 5], ALU.add))
                settle()
                done(dve.tensor_scalar(mom[:, 0, :], mom[:, 0, :], 0.5, None, ALU.mult))
                done(dve.tensor_tensor(mom[:, 3, :], mom[:, 1, :], mom[:, 1, :], ALU.mult))
                settle()
                done(dve.tensor_scalar(mom[:, 4, :], mom[:, 3, :], 0.25, EPS, ALU.mult, ALU.add))
                settle()
                dve.scalar_tensor_tensor(mom[:, 5, :], mom[:, 2, :], 1.0 / D, mom[:, 4, :],
                                         ALU.mult, ALU.add).then_inc(var_ready, 1)
                norms[0] += 1
                dve.wait_ge(std_ready, norms[0])
                done(dve.reciprocal(rstd[:, :], std[:, :]))
                settle()

            def normalise(dst, src, c):
                return dve.tensor_scalar(dst[:, c, :], src[:, c, :], mom[:, 0, c:c + 1], rstd[:, c:c + 1],
                                         ALU.subtract, ALU.mult)

            def norm_groups():
                moments(X)
                for c in range(C):
                    ins = normalise(tok_a, X, c)
                    if c % CQ == CQ - 1:
                        ins.then_inc(norm_ready, 1)

            def residual(f, last):
                moments(f)
                for c in range(C):
                    done(normalise(f, f, c))
                settle()
                for q in range(Q):
                    g = slice(q * CQ, (q + 1) * CQ)
                    ins = dve.tensor_tensor(X[:, g, :], X[:, g, :], f[:, g, :], ALU.add)
                    if last:
                        ins.then_inc(out_ready, 1)
                    else:
                        done(ins)
                settle()

            def ssm(l):
                norm_groups()
                half_v = dtT
                tiles = [(b, h) for b in range(BATCH) for h in range(H)]
                w_buf = yT
                dve.wait_ge(ld_ssm[l], 80)
                dve.wait_ge(a_exp_ready, l + 1)
                dve.tensor_scalar(a_sb[l][:, :, :], a_sb[l][:, :, :], -1.0, None, ALU.mult).then_inc(a_ready, 1)
                for h in range(H):
                    ins = dve.tensor_scalar(ddiag[:, h, :], ident[:, :], dskip_sb[l][:, h:h + 1], None, ALU.mult)
                ins.then_inc(ddiag_ready, 1)
                for b in range(BATCH):
                    i = l * BATCH + b + 1
                    t = slice(b * SEQ, (b + 1) * SEQ)
                    dve.wait_ge(bc_high, i)
                    dve.tensor_tensor(state[:, b, :], ysum[1][:, :], bcT[:, t], ALU.subtract).then_inc(bc_rest, 1)
                    dve.wait_ge(bc_mid, i)
                    dve.tensor_tensor(bcT[96:P, t], state[96:P, b, :], bcT[96:P, t], ALU.subtract).then_inc(bc_ready, 1)
                for i, (b, h) in enumerate(tiles):
                    t = slice(b * SEQ, (b + 1) * SEQ)
                    dve.wait_ge(exp_ready, 8 * l + i + 1)
                    dve.tensor_scalar(w_buf[:, h, t], uT[:, h, t], 1.0, None, ALU.add).then_inc(w_ready, 1)
                    dve.wait_ge(w_ready, 8 * l + i + 1)
                    dve.scalar_tensor_tensor(uT[:, h, t], w_buf[:, h, t], -1.0, uT[:, h, t], ALU.add,
                                             ALU.subtract).then_inc(err_ready, 1)
                for i, (b, h) in enumerate(tiles):
                    t = slice(b * SEQ, (b + 1) * SEQ)
                    dve.wait_ge(ln_ready, 8 * l + i + 1)
                    done(dve.scalar_tensor_tensor(dtT[:, h, t], dtT[:, h, t], 0.0, w_buf[:, h, t], ALU.max, ALU.add))
                    settle()
                    dve.tensor_tensor(dtT[:, h, t], dtT[:, h, t], uT[:, h, t], ALU.subtract).then_inc(dt_ready, 1)
                    dve.wait_ge(dt_ready, 8 * l + i + 1)
                    done(dve.tensor_tensor(uT[:, h, t], dtT[:, h, t], feat_a[:, h, t], ALU.mult))
                settle()
                base = l * BATCH * UNITS
                with dve.Fori(0, BATCH) as b:
                    for u in range(UNITS + 1):
                        n, h = u // H, u % H
                        if u < UNITS:
                            if h == 0:
                                dve.wait_ge(brep_ready, b * N + (l * BATCH * N + n + 1))
                            dve.wait_ge(state_free, b * UNITS + (base + u + 1))
                            dve.tensor_tensor(state[:, u % STATE_RING, :], uT[:, h, bass.ds(b * SEQ, SEQ)],
                                              brep[n % REP][:, :], ALU.mult).then_inc(b_ready, 1)
                        if u:
                            v = u - 1
                            dve.wait_ge(b_ready, b * UNITS + (base + u))
                            dve.wait_ge(abar_ready, b * UNITS + (base + u))
                            s = state[:, v % STATE_RING, :]
                            dve.tensor_tensor_scan(s, abar[:, v % ABAR_RING, :], s, 0.0, ALU.mult,
                                                   ALU.add).then_inc(h_ready, 1)
                dve.wait_ge(tr_copied, TR_AFTER_Y[l])
                residual(f_tok, False)

            TR_AFTER_Y = [16, 8 * 3 + 16]

            dve.memset(zeros[:, :], 0.0).then_inc(zeros_ready, 1)
            dve.memset(ones[:, :], 1.0)
            dve.wait_ge(ld_x, 16)
            dve.wait_ge(ld_const, 32)
            dve.tensor_copy(spread_bf[:, :], spread_f[:, :])
            dve.tensor_copy(ident_bf[:, :], ident[:, :]).then_inc(fsign_in, 1)
            ssm(0)
            moments(X)
            for c in range(C):
                done(normalise(tok_a, X, c))
            settle()
            moments(tok_a)
            for c in range(C):
                done(normalise(tok_a, tok_a, c))
            settle()
            dve.wait_ge(ld_ffn, 80)
            for q in range(Q):
                g = slice(q * CQ, (q + 1) * CQ)
                gb = gamma_sb[:, :].unsqueeze(1).to_broadcast([P, CQ, D])
                bb = beta_sb[:, :].unsqueeze(1).to_broadcast([P, CQ, D])
                done(dve.tensor_tensor(tok_a[:, g, :], tok_a[:, g, :], gb, ALU.mult))
                settle()
                dve.tensor_tensor(tok_a[:, g, :], tok_a[:, g, :], bb, ALU.add).then_inc(xsign_in, 1)
            for h in range(H):
                done(dve.bn_stats(st6[:, h, :], fw_sb[:, h, :]))
            settle()
            done(dve.tensor_tensor(mom[:, 0, 0:H], st6[:, 0:H, 1], st6[:, 0:H, 4], ALU.add))
            settle()
            done(dve.tensor_scalar(mom[:, 0, 0:H], mom[:, 0, 0:H], 0.5, None, ALU.mult))
            settle()
            for h in range(H):
                ins = dve.tensor_scalar(fw_sb[:, h, :], fw_sb[:, h, :], mom[:, 0, h:h + 1], None, ALU.subtract)
            ins.then_inc(fsign_in, 1)
            for c in range(C):
                dve.wait_ge(ffn_ready, c + 1)
                dve.tensor_tensor(f_tok[:, c, :], work[c % 2][:, 0:D], bias_sb[:, :], ALU.add).then_inc(ffn_used, 1)
                dve.wait_ge(ffn_used, c + 1)
                done(dve.tensor_tensor(f_tok[:, c, :], f_tok[:, c, :], alpha_sb[:, :], ALU.mult))
            settle()
            residual(f_tok, False)
            ssm(1)
            norm_groups()
            dve.wait_ge(ld_gate, 48)
            dve.wait_ge(gate_ready, 1)
            logits = work[0][:, 0:C * E].rearrange("p (c e) -> p c e", c=C)
            done(dve.tensor_reduce(psum_e[:, :], logits, AX.X, ALU.max))
            settle()
            dve.tensor_tensor(probs[:, :, :], logits, psum_e[:, :].unsqueeze(2).to_broadcast([P, C, E]),
                              ALU.subtract).then_inc(sm_in, 1)
            dve.wait_ge(sm_out, 1)
            done(dve.tensor_reduce(psum_e[:, :], probs[:, :, :], AX.X, ALU.add))
            settle()
            done(dve.reciprocal(psum_e[:, :], psum_e[:, :]))
            settle()
            done(dve.tensor_tensor(probs[:, :, :], probs[:, :, :], psum_e[:, :].unsqueeze(2).to_broadcast([P, C, E]),
                                   ALU.mult))
            settle()
            for c in range(C):
                done(dve.max(top8[:, c, :], probs[:, c, :]))
            settle()
            for c in range(C):
                done(dve.max_index(top8i[:, c, :], top8[:, c, :], probs[:, c, :]))
            settle()
            done(dve.tensor_copy(top8f[:, :, :], top8i[:, :, 0:2]))
            settle()
            for k in range(2):
                done(dve.tensor_tensor(onehot[k], iota_e.unsqueeze(1).to_broadcast([P, C, E]),
                                       top8f[:, :, k:k + 1].to_broadcast([P, C, E]), ALU.is_equal))
            settle()
            dve.tensor_tensor(picked, onehot[0], onehot[1], ALU.add).then_inc(onehot_ready, 1)
            dve.wait_ge(prefix_ready, 1)
            done(dve.tensor_copy(chunk_count, work[1][:, 0:C * E].rearrange("p (c e) -> p e c", c=C)))
            settle()
            done(dve.tensor_tensor_scan(chunk_end.rearrange("p e c -> p (e c)"), not_first,
                                        chunk_count.rearrange("p e c -> p (e c)"), 0.0, ALU.mult, ALU.add))
            settle()
            done(dve.tensor_tensor(more_rows, chunk_end[:, :, C - 1:C].to_broadcast([P, E, E]),
                                   iota_rows.unsqueeze(1).to_broadcast([P, E, E]), ALU.is_gt))
            settle()
            done(dve.tensor_tensor(chunk_end, chunk_end, chunk_count, ALU.subtract))
            done(dve.tensor_reduce(tiles_e[:, :], more_rows, AX.X, ALU.add))
            settle()
            done(dve.tensor_tensor_scan(tile_end[:, :], ones[:, 0:E], tiles_e[:, :], 0.0, ALU.mult, ALU.add))
            settle()
            done(dve.tensor_tensor(row0[:, :], tile_end[:, :], tiles_e[:, :], ALU.subtract))
            done(dve.tensor_tensor(past_end, tile_end[:, :].unsqueeze(1).to_broadcast([P, TILES, E]),
                                   iota_tile.unsqueeze(2).to_broadcast([P, TILES, E]), ALU.is_le))
            settle()
            done(dve.tensor_scalar(row0[:, :], row0[:, :], float(P), None, ALU.mult))
            done(dve.tensor_reduce(tile_ef[:, :], past_end, AX.X, ALU.add))
            settle()
            dve.tensor_scalar(tile_e[:, :], tile_ef[:, :], float(E - 1), None, ALU.min).then_inc(experts_ready, 1)
            done(dve.tensor_tensor(chunk_end, chunk_end, row0[:, :].unsqueeze(2).to_broadcast([P, E, C]), ALU.add))
            settle()
            done(dve.tensor_tensor(slot, work[0][:, 0:C * E].rearrange("p (c e) -> p c e", c=C),
                                   chunk_end.rearrange("p e c -> p c e"), ALU.add))
            settle()
            for k in range(2):
                done(dve.tensor_tensor(slot_k, slot, onehot[k], ALU.mult))
                settle()
                done(dve.tensor_reduce(slot_f[:, k, :], slot_k, AX.X, ALU.add))
                settle()
                dve.tensor_copy(slot_u[k][:, :], slot_f[:, k, :]).then_inc(slots_ready, 1)

            def shared(lo, hi):
                for i in range(2 * lo, 2 * hi):
                    dve.wait_ge(silu_ready, i + 1)
                    dve.tensor_tensor(gated[:, i % 2, :], silu[:, i % 2, :], bank[i % 2][:, INTER:2 * INTER],
                                      ALU.mult).then_inc(gated_ready, 1)

            def tile_in(at, i):
                dve.wait_ge(xt_ready, at(i + 1))
                dve.tensor_copy(tile_xT[:, i % 2].rearrange("p h t -> p (h t)"), work[i % 2][:, 0:D]).then_inc(xt_copied, 1)

            def tile_gate(at, i):
                dve.wait_ge(tsilu_ready, at(i + 1))
                dve.tensor_tensor(gated[:, i % 2, :], silu[:, i % 2, :], bank[i % 2][:, INTER:2 * INTER],
                                  ALU.mult).then_inc(tgated_ready, 1)

            def tile_out(at, i):
                if i >= LOADS:
                    dve.wait_ge(y_stored[i % LOADS], at.stored(i))
                dve.wait_ge(ty_ready, at(i + 1))
                dve.tensor_copy(tile_y[:, i % LOADS, :], ysum[i % 2][:, 0:D]).then_inc(ty_copied, 1)

            def tile_step(at, i):
                if i >= 0:
                    tile_gate(at, i)
                if i + 2 < TILES:
                    tile_in(at, i + 2)
                if i >= 1:
                    tile_out(at, i - 1)

            shared(0, C // 2)
            run_tiles(dve, tile_step)
            tile_out(Tile(), TILES - 1)
            shared(C // 2, C)
            dve.wait_ge(moe_copied, C)
            for k in range(2):
                dve.wait_ge(y_gathered[k], 16 * C)
                for c in range(C):
                    done(dve.scalar_tensor_tensor(f_moe[:, c, :], y_k[k][:, c, :], top8[:, c, k:k + 1], f_moe[:, c, :],
                                                  ALU.mult, ALU.add))
                settle()
            residual(f_moe, True)

        @block.scalar
        def _(act):
            roots = [0]
            groups = [0]

            def root():
                roots[0] += 1
                act.wait_ge(var_ready, roots[0])
                act.activation(std[:, :], mom[:, 5, :], ACT.Sqrt).then_inc(std_ready, 1)

            def copy_groups(dst):
                for q in range(Q):
                    for h in range(H):
                        i = groups[0]
                        act.wait_ge(tr_ready, i + 1)
                        act.activation(dst(q, h), work[i % 2][:, :], ACT.Copy).then_inc(tr_copied, 1)
                        groups[0] += 1

            def feature_major(q, h):
                return feat_a[:, h, q * CQ * P:(q + 1) * CQ * P]

            def ssm(l):
                act.wait_ge(ld_ssm[l], 80)
                act.activation(a_sb[l][:, :, :], a_sb[l][:, :, :], ACT.Exp).then_inc(a_exp_ready, 1)
                root()
                copy_groups(feature_major)
                for b in range(BATCH):
                    t = slice(b * SEQ, (b + 1) * SEQ)
                    act.wait_ge(proj_ready, 8 * l + 2 * b + 1)
                    act.activation(dtpT[0:RANK[l], t], ysum[0][0:RANK[l], :], ACT.Copy).then_inc(proj_copied, 1)
                    act.wait_ge(proj_ready, 8 * l + 2 * b + 2)
                    act.activation(bcT[:, t], ysum[1][:, :], ACT.Copy).then_inc(bc_high, 1)
                    act.wait_ge(bc_rest, l * BATCH + b + 1)
                    act.activation(bcT[64:P, t], state[64:P, b, :], ACT.Copy).then_inc(bc_mid, 1)
                tiles = [(b, h) for b in range(BATCH) for h in range(H)]
                for i, (b, h) in enumerate(tiles):
                    t = slice(b * SEQ, (b + 1) * SEQ)
                    act.wait_ge(pre_ready, 8 * l + i + 1)
                    act.activation(dtT[:, h, t], work[i % 2][:, :], ACT.Identity, bias=bdt_sb[l][:, h:h + 1])
                    act.activation(uT[:, h, t], work[i % 2][:, :], ACT.Abs, bias=bdt_sb[l][:, h:h + 1])\
                       .then_inc(pre_used, 1)
                    act.wait_ge(pre_used, 8 * l + i + 1)
                    act.activation(uT[:, h, t], uT[:, h, t], ACT.Exp, scale=-1.0).then_inc(exp_ready, 1)
                for i, (b, h) in enumerate(tiles):
                    t = slice(b * SEQ, (b + 1) * SEQ)
                    act.wait_ge(err_ready, 8 * l + i + 1)
                    act.activation(yT[:, h, t], yT[:, h, t], ACT.Ln).then_inc(ln_ready, 1)
                act.wait_ge(a_ready, l + 1)
                act.wait_ge(dt_ready, 8 * (l + 1))
                base = l * BATCH * UNITS
                nbase = l * BATCH * N
                with act.Fori(0, BATCH) as b:
                    for n in range(N):
                        if n * H >= ABAR_RING:
                            act.wait_ge(h_ready, b * UNITS + (base + (n + 1) * H - ABAR_RING))
                        act.wait_ge(crep_ready, b * N + (nbase + n + 1))
                        if n >= CREP_RING:
                            act.wait_ge(hc_ready, b * UNITS + (base + H * (n - CREP_RING + 1)))
                        act.activation(crep[:, n % CREP_RING, :], cps[n % REP][:, :], ACT.Copy)\
                           .then_inc(crep_copied, 1)
                        for h in range(H):
                            u = n * H + h
                            act.activation(abar[:, u % ABAR_RING, :], dtT[:, h, bass.ds(b * SEQ, SEQ)], ACT.Exp,
                                           scale=a_sb[l][:, h, n:n + 1]).then_inc(abar_ready, 1)
                    act.wait_ge(state_free, b * UNITS + (base + UNITS + STATE_RING))
                    act.nop()
                    for h in range(H):
                        act.activation(yT[:, h, bass.ds(b * SEQ, SEQ)], ysum[h][:, :], ACT.Copy)\
                           .then_inc(ysum_free, 1)
                for q in range(Q):
                    for h in range(H):
                        i = groups[0]
                        act.wait_ge(tr_ready, i + 1)
                        act.activation(f_tok[:, q * CQ + 2 * h:q * CQ + 2 * h + 2, :],
                                       work[i % 2][:, :].rearrange("p (c d) -> p c d", c=2), ACT.Copy)\
                           .then_inc(tr_copied, 1)
                        groups[0] += 1
                root()

            ssm(0)
            root()
            root()
            for q in range(Q):
                g = slice(q * CQ, (q + 1) * CQ)
                act.wait_ge(xsign_in, q + 1)
                act.activation(a_sign[:, g, :], tok_a[:, g, :], ACT.Sign).then_inc(xsign_out, 1)
            act.wait_ge(fsign_in, 2)
            act.activation(fw_sign[:, :, :], fw_sb[:, :, :], ACT.Sign).then_inc(fsign_out, 1)
            act.wait_ge(fwT_ready, 1)
            act.activation(fw_signT[:, :, :], work[0][:, 0:D].bitcast(BF16).rearrange("p (h d) -> p h d", h=H),
                           ACT.Copy).then_inc(fwT_copied, 1)
            for q in range(Q):
                for h in range(H):
                    i = groups[0]
                    act.wait_ge(tr_ready, i + 1)
                    act.activation(a_signT[:, h, q * CQ * P:(q + 1) * CQ * P],
                                   work[i % 2][:, 0:CQ * P // 2].bitcast(BF16), ACT.Copy).then_inc(tr_copied, 1)
                    groups[0] += 1
            root()
            ssm(1)
            root()
            copy_groups(feature_major)
            act.wait_ge(sm_in, 1)
            act.activation(probs[:, :, :], probs[:, :, :], ACT.Exp).then_inc(sm_out, 1)

            def shared(lo, hi):
                for i in range(2 * lo, 2 * hi + 2):
                    if i < 2 * hi:
                        act.wait_ge(up_ready, i + 1)
                        act.activation(silu[:, i % 2, :], bank[i % 2][:, 0:INTER], ACT.Silu).then_inc(silu_ready, 1)
                    if 2 * lo <= i - 1 < 2 * hi:
                        act.wait_ge(gT_ready, i)
                        turned_out((i - 1) % 2).then_inc(gT_copied, 1)
                    c = (i - 2) // 2
                    if i % 2 and c >= lo:
                        act.wait_ge(moe_ready, c + 1)
                        act.activation(f_moe[:, c, :], ysum[c % 2][:, 0:D], ACT.Copy).then_inc(moe_copied, 1)

            def turned_out(k):
                act.activation(gatedT[:, k, 0, :], bank[2 + k][:, 0:P], ACT.Copy)
                return act.activation(gatedT[0:IR, k, 1, :], bank[2 + k][0:IR, P:2 * P], ACT.Copy)

            def tile_step(at, i):
                if 0 <= i + 1 < TILES:
                    act.wait_ge(tup_ready, at(i + 2))
                    act.activation(silu[:, (i + 1) % 2, :], bank[(i + 1) % 2][:, 0:INTER], ACT.Silu).then_inc(tsilu_ready, 1)
                if i >= 0:
                    act.wait_ge(tgT_ready, at(i + 1))
                    turned_out(i % 2).then_inc(tgT_copied, 1)

            shared(0, C // 2)
            run_tiles(act, tile_step)
            shared(C // 2, C)
            root()

        @block.gpsimd
        def _(pool):
            for l in range(2):
                pool.wait_ge(ld_ssm[l], 80)
                pool.tensor_copy(bcw_sb[l][:, :, :, :], win_sb[l][:, :, RANK[l]:].unsqueeze(2).to_broadcast([P, H, 4, 2 * N]))\
                    .then_inc(bcw_ready, 1)
            for l in range(2):
                base, nbase = l * BATCH * UNITS, l * BATCH * N
                with pool.Fori(0, BATCH) as b:
                    for u in range(UNITS):
                        n, h = u // H, u % H
                        if h == 0:
                            pool.wait_ge(crep_copied, b * N + (nbase + n + 1))
                        pool.wait_ge(h_ready, b * UNITS + (base + u + 1))
                        s = state[:, u % STATE_RING, :]
                        pool.tensor_tensor(s, s, crep[:, n % CREP_RING, :], ALU.mult).then_inc(hc_ready, 1)
            pool.wait_ge(sorted_zeroed, 16)
            for k in range(2):
                pool.wait_ge(slots_ready, k + 1)
                for c in range(C):
                    pool.indirect_dma_start(out=x_sorted, out_offset=bass.IndirectOffsetOnAxis(ap=slot_u[k][:, c:c + 1], axis=0),
                                            in_=tok_a[:, c, :], in_offset=None).then_inc(sorted_ready, 16)
            pool.wait_ge(sorted_ready, 16 * 2 * C)
            for k in range(LOADS):
                pool.wait_ge(y_stored[k], 16 * TILES // LOADS)
            for k in range(2):
                for c in range(C):
                    pool.indirect_dma_start(out=y_k[k][:, c, :], out_offset=None, in_=y_sorted,
                                            in_offset=bass.IndirectOffsetOnAxis(ap=slot_u[k][:, c:c + 1], axis=0))\
                        .then_inc(y_gathered[k], 16)

        @block.tensor
        def _(pe):
            groups = [0]
            normed = [0]

            def transposes(src, eye_sb, width):
                for q in range(Q):
                    yield q
                    for h in range(H):
                        i = groups[0]
                        if i >= 2:
                            pe.wait_ge(tr_copied, i - 1)
                        o = work[i % 2]
                        o = o[:, 0:CQ * P // 2].bitcast(BF16) if width == 2 else o[:, :]
                        for k in range(CQ):
                            ins = pe.transpose(o[:, k * P:(k + 1) * P], src[:, q * CQ + k, h * P:(h + 1) * P], eye_sb[:, :])
                        ins.then_inc(tr_ready, 1)
                        groups[0] += 1

            def norm_transposes():
                for q in transposes(tok_a, ident, 4):
                    pe.wait_ge(norm_ready, normed[0] + q + 1)
                normed[0] += Q

            def ssm(l):
                pe.wait_ge(ld_const, 32)
                norm_transposes()
                r = RANK[l]
                pe.wait_ge(ld_ssm[l], 80)
                pe.wait_ge(bcw_ready, l + 1)
                for b in range(BATCH):
                    t = slice(b * SEQ, (b + 1) * SEQ)
                    pe.wait_ge(tr_copied, groups[0] - 2 * (Q - 1 - b))
                    if b or l:
                        pe.wait_ge(proj_copied, l * BATCH + b)
                        pe.wait_ge(bc_rest, l * BATCH + b)
                    if l:
                        pe.wait_ge(ysum_free, H + H * BATCH)
                    for h in range(H):
                        ins = pe.matmul(ysum[0][0:r, :], win_sb[l][:, h, 0:r], feat_a[:, h, t], start=h == 0, stop=h == H - 1)
                    ins.then_inc(proj_ready, 1)
                    for h in range(H):
                        ins = pe.matmul(ysum[1][:, :], bcw_sb[l][:, h].rearrange("p k j -> p (k j)"), feat_a[:, h, t],
                                        start=h == 0, stop=h == H - 1)
                    ins.then_inc(proj_ready, 1)
                for b in range(BATCH):
                    t = slice(b * SEQ, (b + 1) * SEQ)
                    pe.wait_ge(proj_copied, l * BATCH + b + 1)
                    for h in range(H):
                        i = 8 * l + 2 * b + h
                        if i % 8 >= 2:
                            pe.wait_ge(pre_used, i - 1)
                        pe.matmul(work[i % 2][:, :], wdt_sb[l][:, h * P:(h + 1) * P], dtpT[0:r, t],
                                  start=True, stop=True).then_inc(pre_ready, 1)
                base, nbase = l * BATCH * UNITS, l * BATCH * N
                pe.wait_ge(bc_ready, (l + 1) * BATCH)
                pe.wait_ge(ddiag_ready, l + 1)
                pe.wait_ge(pre_used, 8 * (l + 1))

                def replicate(b, n):
                    rhs = bcT[:, bass.ds(b * SEQ, SEQ)]
                    pe.matmul(brep[n % REP][:, :], spread_bf[:, n:n + 1].to_broadcast([P, P]), rhs,
                              start=True, stop=True).then_inc(brep_ready, 1)
                    pe.matmul(cps[n % REP][:, :], spread_bf[:, N + n:N + n + 1].to_broadcast([P, P]), rhs,
                              start=True, stop=True).then_inc(crep_ready, 1)

                with pe.Fori(0, BATCH) as b:
                    for n in range(REP):
                        replicate(b, n)
                    for h in range(H):
                        pe.wait_ge(ysum_free, b * H + (l * BATCH * H + h + 1))
                        pe.matmul(ysum[h][:, :], ddiag[:, h, :], feat_a[:, h, bass.ds(b * SEQ, SEQ)], start=True, stop=False)
                    for n in range(N):
                        for h in range(H):
                            u = n * H + h
                            pe.wait_ge(hc_ready, b * UNITS + (base + u + 1))
                            pe.matmul(ysum[h][:, :], ident[:, :], state[:, u % STATE_RING, :], start=False,
                                      stop=n == N - 1).then_inc(state_free, 1)
                        if n + REP < N:
                            replicate(b, n + REP)
                for q in range(Q):
                    pe.wait_ge(ysum_free, H + (l * BATCH + q + 1) * H)
                    for j in range(2):
                        i = groups[0]
                        pe.wait_ge(tr_copied, i - 1)
                        for k in range(2):
                            c = q * CQ + 2 * j + k
                            for h in range(H):
                                ins = pe.transpose(work[i % 2][:, (k * H + h) * P:(k * H + h + 1) * P],
                                                   yT[:, h, c * P:(c + 1) * P], ident[:, :])
                        ins.then_inc(tr_ready, 1)
                        groups[0] += 1

            pe.sem_inc(state_free, STATE_RING)
            pe.sem_inc(ysum_free, H)
            ssm(0)
            pe.wait_ge(fsign_out, 1)
            pe.wait_ge(tr_copied, groups[0])
            for k in range(H):
                for h in range(H):
                    o = work[0][:, 0:D].bitcast(BF16)[:, k * D + h * P:k * D + (h + 1) * P]
                    ins = pe.transpose(o, fw_sign[:, h, k * P:(k + 1) * P], ident_bf[:, :])
            ins.then_inc(fwT_ready, 1)
            pe.wait_ge(fwT_copied, 1)
            for q in transposes(a_sign, ident_bf, 2):
                pe.wait_ge(xsign_out, q + 1)
            pe.wait_ge(tr_copied, groups[0])
            for c in range(C):
                if c >= 2:
                    pe.wait_ge(ffn_used, c - 1)
                for h in range(H):
                    ins = pe.matmul(work[c % 2][:, 0:D], a_signT[:, h, c * P:(c + 1) * P], fw_signT[:, h, :],
                                    start=h == 0, stop=h == H - 1)
                ins.then_inc(ffn_ready, 1)
            pe.wait_ge(ffn_used, C)
            ssm(1)
            norm_transposes()
            pe.wait_ge(tr_copied, groups[0])
            pe.wait_ge(ld_gate, 48)
            for c in range(C):
                for h in range(H):
                    ins = pe.matmul(work[0][:, c * E:(c + 1) * E], feat_a[:, h, c * P:(c + 1) * P], gatew_sb[:, h, :],
                                    start=h == 0, stop=h == H - 1)
            ins.then_inc(gate_ready, 1)
            pe.wait_ge(ld_w13, 16 * H)
            pe.wait_ge(ld_w2, 32)

            pe.wait_ge(onehot_ready, 1)
            flat = picked.rearrange("p c e -> p (c e)")
            pe.matmul(work[0][:, 0:C * E], upper_sb[:, :], flat, start=True, stop=True)
            pe.matmul(work[1][:, 0:C * E], ones[:, :], flat, start=True, stop=True).then_inc(prefix_ready, 1)

            def up(xT, e, k):
                for h in range(H):
                    ins = pe.matmul(bank[k][:, 0:2 * INTER], xT[h], w13_sb[:, h, e, :], start=h == 0, stop=h == H - 1)
                return ins

            def turn(k):
                pe.transpose(bank[2 + k][:, 0:P], gated[:, k, 0:P], ident[:, :])
                return pe.transpose(bank[2 + k][0:IR, P:2 * P], gated[:, k, P:INTER], ident[:, :])

            def down(o, e, k, first, last):
                pe.matmul(ysum[o][:, 0:D], gatedT[:, k, 0, :], w2a[:, e, :], start=first, stop=False)
                return pe.matmul(ysum[o][:, 0:D], gatedT[0:IR, k, 1, :], w2b[:, e, :], start=False, stop=last)

            def shared(lo, hi):
                for i in range(2 * lo, 2 * hi + 2):
                    if i < 2 * hi:
                        if i >= 2:
                            pe.wait_ge(gated_ready, i - 1)
                        c = i // 2
                        up([feat_a[:, h, c * P:(c + 1) * P] for h in range(H)], E + i % 2, i % 2).then_inc(up_ready, 1)
                    if 2 * lo <= i - 1 < 2 * hi:
                        pe.wait_ge(gated_ready, i)
                        turn((i - 1) % 2).then_inc(gT_ready, 1)
                    if i - 2 >= 2 * lo:
                        j = i - 2
                        c = j // 2
                        pe.wait_ge(gT_copied, j + 1)
                        if j % 2 == 0 and c >= 2:
                            pe.wait_ge(moe_copied, c - 1)
                        ins = down(c % 2, E + j % 2, j % 2, j % 2 == 0, j % 2 == 1)
                        if j % 2:
                            ins.then_inc(moe_ready, 1)

            def expert(at, i):
                return pe.value_load(tile_e[0:1, at.slice(i)], min_val=0, max_val=E - 1)

            def tile_step(at, i):
                e_up = expert(at, i + 1) if 0 <= i + 1 < TILES else None
                e_down = expert(at, i - 1) if i >= 1 else None
                if i + 2 < TILES:
                    j = i + 2
                    pe.wait_ge(x_loaded[j % LOADS], at.loaded(j))
                    if j >= 2:
                        pe.wait_ge(xt_copied, at(j - 1))
                    for h in range(H):
                        ins = pe.transpose(work[j % 2][:, h * P:(h + 1) * P], tile_x[:, j % LOADS, h * P:(h + 1) * P], ident[:, :])
                    ins.then_inc(xt_ready, 1)
                if 0 <= i + 1 < TILES:
                    if i >= 1:
                        pe.wait_ge(tgated_ready, at(i))
                    pe.wait_ge(xt_copied, at(i + 2))
                    up([tile_xT[:, (i + 1) % 2, h, :] for h in range(H)], bass.ds(e_up, 1), (i + 1) % 2).then_inc(tup_ready, 1)
                if i >= 0:
                    pe.wait_ge(tgated_ready, at(i + 1))
                    turn(i % 2).then_inc(tgT_ready, 1)
                if i >= 1:
                    tile_down(at, i - 1, e_down)

            def tile_down(at, i, e):
                if i >= 2:
                    pe.wait_ge(ty_copied, at(i - 1))
                pe.wait_ge(tgT_copied, at(i + 1))
                down(i % 2, bass.ds(e, 1), i % 2, True, True).then_inc(ty_ready, 1)

            pe.wait_ge(ld_w13, 16 * H)
            pe.wait_ge(ld_w2, 32)
            shared(0, C // 2)
            pe.wait_ge(moe_copied, C // 2)
            pe.wait_ge(experts_ready, 1)
            run_tiles(pe, tile_step)
            tile_down(Tile(), TILES - 1, expert(Tile(), TILES - 1))
            pe.wait_ge(ty_copied, TILES)
            shared(C // 2, C)


class Tile:

    def __init__(self, m=None):
        self.m = m

    def __call__(self, i):
        return i if self.m is None else self.m * LOADS + i

    def loaded(self, i):
        n = 16 * (i // LOADS + 1)
        return n if self.m is None else self.m * 16 + n

    def stored(self, i):
        n = 16 * (i // LOADS)
        return n if self.m is None else self.m * 16 + n

    def slice(self, i):
        return slice(i, i + 1) if self.m is None else bass.ds(self.m * LOADS + i, 1)


def run_tiles(engine, step):
    first = LOADS + 2
    rounds = (TILES - 2 - first) // LOADS
    for i in range(-2, first):
        step(Tile(), i)
    with engine.Fori(0, rounds) as m:
        for k in range(LOADS):
            step(Tile(m), first + k)
    for i in range(first + rounds * LOADS, TILES):
        step(Tile(), i)


def kernel(**inputs):
    import numpy as np
    import concourse.bacc as bacc
    from concourse import mybir as mb
    from concourse.bass_utils import run_bass_kernel_spmd as launch

    i = {k: np.asarray(v) for k, v in inputs.items()}
    sw1, sw3 = (i[f"L1_ffn_{n}"].reshape(ES - E, INTER, D) for n in ("sw1", "sw3"))
    sw2 = i["L1_ffn_sw2"].reshape(D, ES - E, INTER).transpose(1, 0, 2)
    w1, w3, w2 = (np.concatenate([i[f"L1_ffn_{n}"], s]) for n, s in (("w1", sw1), ("w3", sw3), ("w2", sw2)))
    arrays = {
        "x": i["L0_attn_x"].reshape(T, D),
        "eye": np.eye(P, dtype=np.float32),
        "spread": np.concatenate([np.eye(2 * N), 0 * np.eye(2 * N), np.eye(2 * N), np.eye(2 * N)]).astype(np.float32),
        "a_log0": i["L0_attn_A_log"], "a_log1": i["L1_attn_A_log"],
        "d_skip0": i["L0_attn_D"].reshape(H, P).T, "d_skip1": i["L1_attn_D"].reshape(H, P).T,
        "w_in0": i["L0_attn_W_xproj"].T,
        "w_in1": np.concatenate([i["L1_attn_W_delta"], i["L1_attn_W_B"], i["L1_attn_W_C"]], axis=1),
        "w_dt0": i["L0_attn_W_dt"].T, "w_dt1": i["L1_attn_W_dt"],
        "b_dt0": i["L0_attn_b_dt"].reshape(H, P).T, "b_dt1": i["L1_attn_b_dt"].reshape(H, P).T,
        "gamma": i["L0_ffn_gamma"], "beta": i["L0_ffn_beta"], "weight": i["L0_ffn_weight"],
        "bias": i["L0_ffn_bias"], "alpha": i["L0_ffn_alpha"],
        "gate_wt": i["L1_ffn_gate_w"].T, "upper": np.triu(np.ones((P, P), np.float32), 1),
        "counts": np.concatenate([np.arange(E), P * np.arange(E), np.arange(TILES),
                                  np.arange(E * C) % C != 0]).astype(np.float32),
        "w13": np.concatenate([w1, w3], axis=1).transpose(0, 2, 1), "w2": w2.transpose(0, 2, 1),
    }
    arrays = {k: np.ascontiguousarray(v) for k, v in arrays.items()}
    nc = bacc.Bacc("TRN2", target_bir_lowering=False, num_devices=1)
    ap = {k: nc.dram_tensor(k, v.shape, mb.dt.from_np(v.dtype), kind="ExternalInput").ap() for k, v in arrays.items()}
    for k in ("a_log", "d_skip", "w_in", "w_dt", "b_dt"):
        ap[k] = [ap.pop(f"{k}{l}") for l in range(2)]
    ap["out"] = nc.dram_tensor("out", (T, D), F32, kind="ExternalOutput").ap()
    for k in ("x_sorted", "y_sorted"):
        ap[k] = nc.dram_tensor(k, (TILES * P, D), F32, kind="Internal").ap()
    sandwich_kernel(nc, **ap)
    r = launch(nc, [arrays], core_ids=[0])
    return r.results[0]["out"].reshape(BATCH, SEQ, D)
```

```python
import concourse.bass as bass
from concourse import mybir
from contextlib import ExitStack

F32 = mybir.dt.float32
BF16 = mybir.dt.bfloat16
U32 = mybir.dt.uint32
ALU = mybir.AluOpType
ACT = mybir.ActivationFunctionType
AX = mybir.AxisListType

P = 128
D = 256
H = D // P
BATCH, SEQ = 4, 512
T = BATCH * SEQ
C = T // P
CQ = 4
Q = C // CQ
N = 16
RANK = (64, 128)
E = 16
ES = 18
INTER = 176
IR = INTER - P
EPS = 1e-5
UNITS = N * H
STATE_RING, ABAR_RING, CREP_RING = 8, 2, 4
TILES = 2 * T // P + E - 1
LOADS = 4
AHEAD = 2
SHARED_FIRST = 10
REP = 2


def sandwich_kernel(nc, x, eye, spread, a_log, d_skip, w_in, w_dt, b_dt, gamma, beta, weight, bias, alpha,
                    gate_wt, upper, counts, w13, w2, x_sorted, y_sorted, out):
    ctx = ExitStack()
    with ctx:
        def sb(name, shape, dt=F32):
            return ctx.enter_context(nc.sbuf_tensor(name, shape, dt))

        def sem(name):
            return ctx.enter_context(nc.semaphore(name))

        X = sb("residual", [P, C, D])
        tok_a = sb("tok_a", [P, C, D])
        feat_a = sb("feat_a", [P, H, T])
        arena = sb("arena", [P, 3 * H * T // 1])
        dtT = arena[:, 0:H * T].rearrange("p (h t) -> p h t", h=H)
        uT = arena[:, H * T:2 * H * T].rearrange("p (h t) -> p h t", h=H)
        state = arena[:, 2 * H * T:2 * H * T + STATE_RING * SEQ].rearrange("p (r t) -> p r t", r=STATE_RING)
        w2a = arena[:, 0:ES * D].rearrange("p (e d) -> p e d", e=ES)
        w2b = arena[0:IR, ES * D:2 * ES * D].rearrange("p (e d) -> p e d", e=ES)
        yT = tok_a[:, :, :].rearrange("p c d -> p (c d)").rearrange("p (h t) -> p h t", h=H)
        ring_end = 2 * CREP_RING * SEQ
        rings = sb("rings", [P, ring_end + 2 * T])
        crep = rings[:, 0:CREP_RING * SEQ].rearrange("p (r t) -> p r t", r=CREP_RING)
        bcT = rings[:, ring_end:ring_end + T // 2].bitcast(BF16)
        dtpT = rings[:, ring_end + T:ring_end + 2 * T]
        f_moe = rings[:, 0:C * D].rearrange("p (c d) -> p c d", c=C)
        tile_x = rings[:, C * D:C * D + LOADS * D].rearrange("p (r d) -> p r d", r=LOADS)
        tile_y = rings[:, C * D + LOADS * D:C * D + 2 * LOADS * D].rearrange("p (r d) -> p r d", r=LOADS)
        tile_xT = rings[:, C * D + 2 * LOADS * D:C * D + (2 * LOADS + 2) * D]\
            .rearrange("p (r h t) -> p r h t", r=2, h=H)
        w13_sb = sb("w13_sb", [P, H, ES, 2 * INTER])
        ident = sb("ident", [P, P])
        spread_f = sb("spread_f", [P, 2 * N])
        spread_bf = sb("spread_bf", [P, 2 * N], BF16)
        bcw_sb = [sb(f"bcw_sb{l}", [P, H, 4, 2 * N]) for l in range(2)]
        ident_bf = sb("ident_bf", [P, P], BF16)
        a_sb = [sb(f"a_sb{l}", [P, H, N]) for l in range(2)]
        dskip_sb = [sb(f"dskip_sb{l}", [P, H]) for l in range(2)]
        ddiag = sb("ddiag", [P, H, P])
        win_sb = [sb(f"win_sb{l}", [P, H, RANK[l] + 2 * N]) for l in range(2)]
        wdt_sb = [sb(f"wdt_sb{l}", [RANK[l], D]) for l in range(2)]
        bdt_sb = [sb(f"bdt_sb{l}", [P, H]) for l in range(2)]
        gamma_sb, beta_sb, bias_sb, alpha_sb = (sb(f"{n}_sb", [P, H]) for n in ("gamma", "beta", "bias", "alpha"))
        fw_sb = sb("fw_sb", [P, H, D])
        fw_sign = sb("fw_sign", [P, H, D], BF16)
        fw_signT = sb("fw_signT", [P, H, D], BF16)
        gatew_sb = sb("gatew_sb", [P, H, E])
        upper_sb = sb("upper_sb", [P, P])
        ones = sb("ones", [P, P])
        zeros = sb("zeros", [P, D])
        counts_sb = sb("counts_sb", [P, 2 * E + TILES + E * C])
        iota_e = counts_sb[:, 0:E]
        iota_rows = counts_sb[:, E:2 * E]
        iota_tile = counts_sb[:, 2 * E:2 * E + TILES]
        not_first = counts_sb[:, 2 * E + TILES:]
        route = arena[:, 2 * ES * D:]
        cut = [0]

        def part(*shape):
            size = 1
            for n in shape:
                size *= n
            view = route[:, cut[0]:cut[0] + size]
            cut[0] += size
            return view.rearrange("p (a b) -> p a b", a=shape[0])

        onehot = [part(C, E), part(C, E)]
        picked = part(C, E)
        chunk_count, chunk_end = part(E, C), part(E, C)
        more_rows = part(E, E)
        past_end = part(TILES, E)
        slot = part(C, E)
        slot_k = part(C, E)
        tiles_e, tile_end, row0 = (sb(n, [P, E]) for n in ("tiles_e", "tile_end", "row0"))
        slot_f = sb("slot_f", [P, 2, C])
        slot_u = [sb(f"slot_u{k}", [P, C], U32) for k in range(2)]
        tile_ef = sb("tile_ef", [P, TILES])
        tile_e = sb("tile_e", [P, TILES], U32)
        y_k = [tok_a, w13_sb[:, 0].rearrange("p e i -> p (e i)")[:, 0:C * D].rearrange("p (c d) -> p c d", c=C)]
        st6 = sb("st6", [P, C, 6])
        mom = sb("mom", [P, C, 2])
        std = sb("std", [P, C])
        rstd, shift = sb("rstd", [P, C]), sb("shift", [P, C])
        eps_sb = sb("eps_sb", [P, 1])
        probs = sb("probs", [P, C, E])
        row = sb("row", [P, C])
        top8 = sb("top8", [P, C, 8])
        top8i = sb("top8i", [P, C, 8], U32)
        top2 = sb("top2", [P, C, 2])
        silu = sb("silu", [P, 2, INTER])
        gated = sb("gated", [P, 2, INTER])
        gatedT = sb("gatedT", [P, 2, 2, P])
        early = w13_sb[:, :, :, :].rearrange("p h e i -> p (h e i)")
        f_tok = [early[:, 0:C * D].rearrange("p (c d) -> p c d", c=C),
                 rings[:, ring_end:ring_end + C * D].rearrange("p (c d) -> p c d", c=C)]
        a_signT = early[:, C * D:3 * C * D // 2].bitcast(BF16).rearrange("p (h t) -> p h t", h=H)
        w_buf = early[:, 2 * C * D:3 * C * D].rearrange("p (h t) -> p h t", h=H)

        bank = [ctx.enter_context(nc.psum_tensor(f"bank{i}", [P, 512], F32)) for i in range(8)]
        brep, cps = bank[0:REP], bank[2:2 + REP]
        ysum = bank[4:6]
        work = bank[6:8]
        logits = [b[:, 0:CQ * E].rearrange("p (c e) -> p c e", c=CQ) for b in bank[2:2 + Q]]
        abar = bank[6:6 + ABAR_RING]

        ld_ident, ld_spread, ld_ffn, ld_gate, ld_w13, ld_w2, stored = (
            sem(n) for n in ("ld_ident", "ld_spread", "ld_ffn", "ld_gate", "ld_w13", "ld_w2", "stored"))
        ld_x = [sem(f"ld_x{q}") for q in range(Q)]
        ld_ssm = [sem(f"ld_ssm{l}") for l in range(2)]
        dve_done = sem("dve_done")
        var_ready, std_ready = sem("var_ready"), sem("std_ready")
        scale_ready = sem("scale_ready")
        norm_ready = sem("norm_ready")
        tr_ready, tr_copied = sem("tr_ready"), sem("tr_copied")
        ytr_ready, ytr_copied = sem("ytr_ready"), sem("ytr_copied")
        ftr_ready, ftr_copied = sem("ftr_ready"), sem("ftr_copied")
        y_normed, r_normed, m_normed, y_added, r_added = (
            sem(n) for n in ("y_normed", "r_normed", "m_normed", "y_added", "r_added"))
        g_normed = sem("g_normed")
        scaled, ftok_ready, ftok_copied = sem("scaled"), sem("ftok_ready"), sem("ftok_copied")
        proj_ready, proj_copied = sem("proj_ready"), sem("proj_copied")
        pre_ready, pre_used = sem("pre_ready"), sem("pre_used")
        exp_ready, w_ready, err_ready, ln_ready = (
            sem(n) for n in ("exp_ready", "w_ready", "err_ready", "ln_ready"))
        dt_ready, u_ready = sem("dt_ready"), sem("u_ready")
        a_exp_ready, a_ready, ddiag_ready = sem("a_exp_ready"), sem("a_ready"), sem("ddiag_ready")
        bcw_ready, bc_high, bc_rest, bc_mid, bc_ready = (
            sem(n) for n in ("bcw_ready", "bc_high", "bc_rest", "bc_mid", "bc_ready"))
        brep_ready, crep_ready, crep_copied = sem("brep_ready"), sem("crep_ready"), sem("crep_copied")
        abar_ready, b_ready, h_ready, hc_ready = (
            sem(n) for n in ("abar_ready", "b_ready", "h_ready", "hc_ready"))
        state_free = sem("state_free")
        ysum_free = sem("ysum_free")
        fsign_in, fsign_out, fwT_ready, fwT_copied = (
            sem(n) for n in ("fsign_in", "fsign_out", "fwT_ready", "fwT_copied"))
        ffn_ready = sem("ffn_ready")
        gate_ready, sm_in, sm_out = sem("gate_ready"), sem("sm_in"), sem("sm_out")
        up_ready, silu_ready, gated_ready, gT_ready, gT_copied, moe_ready, moe_copied = (
            sem(n) for n in ("up_ready", "silu_ready", "gated_ready", "gT_ready", "gT_copied", "moe_ready", "moe_copied"))
        onehot_ready, prefix_ready, slots_ready, experts_ready = (
            sem(n) for n in ("onehot_ready", "prefix_ready", "slots_ready", "experts_ready"))
        zeros_ready, sorted_zeroed, sorted_ready = sem("zeros_ready"), sem("sorted_zeroed"), sem("sorted_ready")
        x_loaded = [sem(f"x_loaded{k}") for k in range(LOADS)]
        y_stored = [sem(f"y_stored{k}") for k in range(LOADS)]
        xt_ready, xt_copied, tup_ready, tsilu_ready, tgated_ready, tgT_ready, tgT_copied, ty_ready, ty_copied = (
            sem(n) for n in ("xt_ready", "xt_copied", "tup_ready", "tsilu_ready", "tgated_ready", "tgT_ready",
                             "tgT_copied", "ty_ready", "ty_copied"))
        y_gathered = [sem(f"y_gathered{c}") for c in range(C)]
        out_ready = sem("out_ready")

        into_ssm = ["x_stat", "x_norm", "turn", "proj", "pre", "err"]
        softplus = ["log", "dt"]
        out_of_ssm = ["y_turn", "y_stat", "y_add"]
        ffn = ["f_stat", "g_stat", "f_norm", "f_turn", "f_mm", "f_back", "r_stat", "r_add"]
        routing = ["x_stat", "x_norm", "turn", "gate", "softmax", "pick"]
        combine = [("gates", 3), ("m_add", 0), ("gates", 5), ("m_add", 1), ("gates", C - SHARED_FIRST),
                   ("m_stat", 0), ("m_stat", 1), ("m_add", 2), ("m_norm", 0), ("m_stat", 2), ("m_norm", 1),
                   ("m_add", 3), ("m_out", 0), ("m_stat", 3), ("m_norm", 2), ("m_out", 1), ("m_norm", 3),
                   ("m_out", 2), ("m_out", 3)]

        def norm_of(name, l):
            return {"y_add": (f_tok[l - 1], f_tok[l - 1], y_normed), "f_norm": (tok_a, X, g_normed),
                    "r_add": (f_tok[0], f_tok[0], r_normed), "m_norm": (f_moe, f_moe, m_normed)}[name]

        block = ctx.enter_context(nc.Block())

        @block.sync
        def _(sp):
            for q in range(Q):
                g = slice(q * CQ, (q + 1) * CQ)
                sp.dma_start(X[:, g, :], x.rearrange("(c p) d -> p c d", p=P)[:, g, :]).then_inc(ld_x[q], 16)
                if q == 0:
                    sp.dma_start(ident[:, :], eye).then_inc(ld_ident, 16)
            sp.dma_start(spread_f[:, :], spread).then_inc(ld_spread, 16)
            for l in range(2):
                for dst, src in ((a_sb[l], a_log[l]), (dskip_sb[l], d_skip[l]), (bdt_sb[l], b_dt[l])):
                    view = src.rearrange("(h p) n -> p h n", p=P) if dst is a_sb[l] else src
                    sp.dma_start(dst[:], view).then_inc(ld_ssm[l], 16)
                sp.dma_start(win_sb[l][:, :, :], w_in[l].rearrange("(h p) r -> p h r", p=P)).then_inc(ld_ssm[l], 16)
                sp.dma_start(wdt_sb[l][:, :], w_dt[l]).then_inc(ld_ssm[l], 16)
            sp.dma_start(fw_sb[:, :, :], weight.rearrange("(h p) d -> p h d", p=P)).then_inc(ld_ffn, 16)
            for dst, src in ((gamma_sb, gamma), (beta_sb, beta), (bias_sb, bias), (alpha_sb, alpha)):
                sp.dma_start(dst[:, :], src).then_inc(ld_ffn, 16)
            sp.dma_start(gatew_sb[:, :, :], gate_wt.rearrange("(h p) e -> p h e", p=P)).then_inc(ld_gate, 16)
            sp.dma_start(upper_sb[:, :], upper).then_inc(ld_gate, 16)
            sp.dma_start(counts_sb[:, :], counts.partition_broadcast(P)).then_inc(ld_gate, 16)
            sp.wait_ge(zeros_ready, 1)
            sp.wait_ge(dt_ready, BATCH * H)
            sp.dma_start(x_sorted.rearrange("(t p) d -> p t d", p=P),
                         zeros[:, :].unsqueeze(1).to_broadcast([P, TILES, D])).then_inc(sorted_zeroed, 16)
            sp.wait_ge(dt_ready, 2 * BATCH * H)
            for h in range(H):
                sp.dma_start(w13_sb[:, h], w13[:, h * P:(h + 1) * P, :].rearrange("e p i -> p e i")).then_inc(ld_w13, 16)
            sp.wait_ge(ysum_free, H + 2 * BATCH * H)
            sp.dma_start(w2a, w2[:, 0:P, :].rearrange("e p d -> p e d")).then_inc(ld_w2, 16)
            sp.dma_start(w2b, w2[:, P:INTER, :].rearrange("e p d -> p e d")).then_inc(ld_w2, 16)
            x_tiles = x_sorted.rearrange("(t p) d -> t p d", p=P)
            y_tiles = y_sorted.rearrange("(t p) d -> t p d", p=P)
            sp.wait_ge(sorted_ready, 16 * 2 * C)

            def tile_load(at, i):
                if i >= LOADS:
                    sp.wait_ge(xt_ready, at(i - LOADS + 1))
                sp.dma_start(tile_x[:, i % LOADS, :], x_tiles[at.slice(i)].rearrange("t p d -> (t p) d"))\
                  .then_inc(x_loaded[i % LOADS], 16)

            def tile_store(at, i):
                sp.wait_ge(ty_copied, at(i + 1))
                sp.dma_start(y_tiles[at.slice(i)].rearrange("t p d -> (t p) d"), tile_y[:, i % LOADS, :])\
                  .then_inc(y_stored[i % LOADS], 16)

            lead = LOADS + 3
            rounds = (TILES - lead) // LOADS
            for i in range(lead):
                tile_load(Tile(), i)
            with sp.Fori(0, rounds) as m:
                for i in range(LOADS):
                    tile_load(Tile(m), lead + i)
                    tile_store(Tile(m), i)
            for i in range(rounds * LOADS, TILES):
                if i + lead < TILES:
                    tile_load(Tile(), i + lead)
                tile_store(Tile(), i)
            for c in range(0, C, 2):
                sp.wait_ge(out_ready, c // 2 + 1)
                sp.dma_start(out.rearrange("(c p) d -> p c d", p=P)[:, c:c + 2, :], X[:, c:c + 2, :]).then_inc(stored, 16)
            sp.wait_ge(stored, 16 * C // 2)

        @block.vector
        def _(dve):
            steps = [0]
            norms = [0]
            stat_of = {}

            def done(ins, times=1):
                steps[0] += times
                return ins.then_inc(dve_done, 1)

            def settle():
                dve.wait_ge(dve_done, steps[0])

            def stat(src, q, ready=None, count=0, each=1):
                for c in range(q * CQ, (q + 1) * CQ):
                    j = c - q * CQ
                    if ready is not None and j % each == 0:
                        dve.wait_ge(ready, count + j // each + 1)
                    done(dve.bn_stats(st6[:, c, :], src[:, c, :]))
                settle()
                for c in range(q * CQ, (q + 1) * CQ):
                    ins = dve.bn_aggr(mom[:, c, :], st6[:, c, :])
                ins.then_inc(var_ready, 1)
                norms[0] += 1
                stat_of[q] = norms[0]

            def scale(name, q):
                g = slice(q * CQ, (q + 1) * CQ)
                dve.wait_ge(std_ready, stat_of[q])
                if name == "f_norm":
                    done(dve.reciprocal(std[:, g], std[:, g]))
                    settle()
                    done(dve.tensor_tensor(rstd[:, g], rstd[:, g], std[:, g], ALU.mult))
                else:
                    done(dve.reciprocal(rstd[:, g], std[:, g]))
                settle()
                if name != "x_norm":
                    dve.scalar_tensor_tensor(shift[:, g], mom[:, g, 0], -1.0, rstd[:, g], ALU.mult, ALU.mult)\
                       .then_inc(scale_ready, 1)

            def stage(name, q, l):
                g = slice(q * CQ, (q + 1) * CQ)
                t = slice(q * SEQ, (q + 1) * SEQ)
                k = l * Q + q
                if name == "x_stat":
                    if l == 0:
                        dve.wait_ge(ld_x[q], 16)
                        stat(X, q)
                    elif l == 1:
                        stat(X, q, r_added, q * CQ)
                    else:
                        stat(X, q, y_added, (Q + q) * CQ)
                elif name == "x_norm":
                    if l:
                        dve.wait_ge(ytr_copied, l * Q * H)
                    scale(name, q)
                    for c in range(q * CQ, (q + 1) * CQ):
                        dve.tensor_scalar(tok_a[:, c, :], X[:, c, :], mom[:, c, 0:1], rstd[:, c:c + 1], ALU.subtract,
                                          ALU.mult).then_inc(norm_ready, 1)
                elif name == "proj":
                    dve.wait_ge(bc_high, k + 1)
                    dve.tensor_tensor(state[:, q, :], bank[1][:, :], bcT[:, t], ALU.subtract).then_inc(bc_rest, 1)
                elif name == "pre":
                    dve.wait_ge(bc_mid, k + 1)
                    dve.tensor_tensor(bcT[96:P, t], state[96:P, q, :], bcT[96:P, t], ALU.subtract).then_inc(bc_ready, 1)
                elif name == "err":
                    for h in range(H):
                        i = k * H + h + 1
                        dve.wait_ge(exp_ready, i)
                        dve.tensor_scalar(w_buf[:, h, t], uT[:, h, t], 1.0, None, ALU.add).then_inc(w_ready, 1)
                    for h in range(H):
                        i = k * H + h + 1
                        dve.wait_ge(w_ready, i)
                        dve.scalar_tensor_tensor(uT[:, h, t], w_buf[:, h, t], -1.0, uT[:, h, t], ALU.add,
                                                 ALU.subtract).then_inc(err_ready, 1)
                    for h in range(H):
                        dve.wait_ge(err_ready, k * H + h + 1)
                        done(dve.tensor_tensor(dtT[:, h, t], dtT[:, h, t], uT[:, h, t], ALU.subtract))
                elif name == "dt":
                    settle()
                    for h in range(H):
                        dve.wait_ge(ln_ready, k * H + h + 1)
                        dve.tensor_tensor(dtT[:, h, t], dtT[:, h, t], w_buf[:, h, t], ALU.add).then_inc(dt_ready, 1)
                    for h in range(H - 1):
                        dve.wait_ge(dt_ready, k * H + h + 1)
                        done(dve.tensor_tensor(uT[:, h, t], dtT[:, h, t], feat_a[:, h, t], ALU.mult))
                elif name == "y_stat":
                    stat(f_tok[l - 1], q, ytr_copied, ((l - 1) * Q + q) * 2, 2)
                elif name == "y_add":
                    scale(name, q)
                elif name == "f_stat":
                    stat(X, q, y_added, q * CQ)
                elif name == "g_stat":
                    dve.wait_ge(std_ready, stat_of[q])
                    done(dve.reciprocal(rstd[:, g], std[:, g]))
                    settle()
                    done(dve.tensor_tensor(mom[:, g, 1], mom[:, g, 1], rstd[:, g], ALU.mult))
                    settle()
                    dve.tensor_tensor(mom[:, g, 1], mom[:, g, 1], rstd[:, g], ALU.mult).then_inc(var_ready, 1)
                    norms[0] += 1
                    stat_of[q] = norms[0]
                elif name == "f_norm":
                    scale(name, q)
                elif name == "f_mm":
                    for h in range(H):
                        dve.wait_ge(ffn_ready, q * H + h + 1)
                        dve.tensor_scalar(feat_a[:, h, t], bank[4 + h][:, :], bias_sb[:, h:h + 1], alpha_sb[:, h:h + 1],
                                          ALU.add, ALU.mult).then_inc(scaled, 1)
                elif name == "r_stat":
                    stat(f_tok[0], q, ftok_copied, q * 2, 2)
                elif name == "r_add":
                    scale(name, q)
                elif name == "softmax":
                    dve.wait_ge(gate_ready, q + 1)
                    done(dve.tensor_reduce(row[:, g], logits[q], AX.X, ALU.max))
                    settle()
                    dve.tensor_tensor(probs[:, g, :], logits[q], row[:, g].unsqueeze(2).to_broadcast([P, CQ, E]),
                                      ALU.subtract).then_inc(sm_in, 1)
                elif name == "pick":
                    dve.wait_ge(sm_out, q + 1)
                    done(dve.tensor_reduce(row[:, g], probs[:, g, :], AX.X, ALU.add))
                    settle()
                    done(dve.reciprocal(row[:, g], row[:, g]))
                    settle()
                    done(dve.tensor_tensor(probs[:, g, :], probs[:, g, :], row[:, g].unsqueeze(2).to_broadcast([P, CQ, E]),
                                           ALU.mult))
                    settle()
                    for c in range(q * CQ, (q + 1) * CQ):
                        done(dve.max(top8[:, c, :], probs[:, c, :]))
                    settle()
                    for c in range(q * CQ, (q + 1) * CQ):
                        done(dve.max_index(top8i[:, c, :], top8[:, c, :], probs[:, c, :]))
                    settle()
                    done(dve.tensor_copy(top2[:, g, :], top8i[:, g, 0:2]))
                    settle()
                    if q == 0:
                        dve.wait_ge(ld_gate, 48)
                    for k in range(2):
                        done(dve.tensor_tensor(onehot[k][:, g, :], iota_e.unsqueeze(1).to_broadcast([P, CQ, E]),
                                               top2[:, g, k:k + 1].to_broadcast([P, CQ, E]), ALU.is_equal))
                    settle()
                    dve.tensor_tensor(picked[:, g, :], onehot[0][:, g, :], onehot[1][:, g, :], ALU.add).then_inc(onehot_ready, 1)

            def ssm_weights(l):
                dve.wait_ge(ld_ssm[l], 80)
                dve.wait_ge(a_exp_ready, l + 1)
                dve.tensor_scalar(a_sb[l][:, :, :], a_sb[l][:, :, :], -1.0, None, ALU.mult).then_inc(a_ready, 1)
                for h in range(H):
                    ins = dve.tensor_scalar(ddiag[:, h, :], ident[:, :], dskip_sb[l][:, h:h + 1], None, ALU.mult)
                ins.then_inc(ddiag_ready, 1)

            def scan(l):
                settle()
                base = l * BATCH * UNITS
                with dve.Fori(0, BATCH) as b:
                    for u in range(UNITS + 1):
                        n, h = u // H, u % H
                        if u < UNITS:
                            if h == 0:
                                dve.wait_ge(brep_ready, b * N + (l * BATCH * N + n + 1))
                            if u == H - 1:
                                dve.wait_ge(u_ready, b + (l * BATCH + 1))
                            dve.wait_ge(state_free, b * UNITS + (base + u + 1))
                            dve.tensor_tensor(state[:, u % STATE_RING, :], uT[:, h, bass.ds(b * SEQ, SEQ)],
                                              brep[n % REP][:, :], ALU.mult).then_inc(b_ready, 1)
                        if u:
                            v = u - 1
                            dve.wait_ge(b_ready, b * UNITS + (base + u))
                            dve.wait_ge(abar_ready, b * UNITS + (base + u))
                            s = state[:, v % STATE_RING, :]
                            dve.tensor_tensor_scan(s, abar[v % ABAR_RING][:, :], s, 0.0, ALU.mult,
                                                   ALU.add).then_inc(h_ready, 1)

            dve.memset(zeros[:, :], 0.0).then_inc(zeros_ready, 1)
            dve.memset(ones[:, :], 1.0)
            dve.memset(eps_sb[:, :], EPS)
            for name, q in in_turn(into_ssm):
                stage(name, q, 0)
            dve.wait_ge(ld_spread, 16)
            dve.tensor_copy(spread_bf[:, :], spread_f[:, :])
            dve.wait_ge(ld_ident, 16)
            dve.tensor_copy(ident_bf[:, :], ident[:, :]).then_inc(fsign_in, 1)
            ssm_weights(0)
            for name, q in in_turn(softplus):
                stage(name, q, 0)
            scan(0)
            dve.wait_ge(ld_ffn, 80)
            for h in range(H):
                done(dve.bn_stats(st6[:, h, :], fw_sb[:, h, :]))
            settle()
            for h in range(H):
                done(dve.bn_aggr(mom[:, h, :], st6[:, h, :]))
            settle()
            for h in range(H):
                ins = dve.tensor_scalar(fw_sb[:, h, :], fw_sb[:, h, :], mom[:, h, 0:1], None, ALU.subtract)
            ins.then_inc(fsign_in, 1)
            dve.wait_ge(fsign_in, 2)
            ssm_weights(1)
            for name, q in [*in_turn(out_of_ssm + ffn + into_ssm), *in_turn(softplus)]:
                stage(name, q, 1)
            scan(1)
            for name, q in in_turn(out_of_ssm + routing):
                stage(name, q, 2)
            shared_done = [0]

            def shared_gates(n):
                for i in range(shared_done[0], shared_done[0] + n):
                    dve.wait_ge(silu_ready, i + 1)
                    dve.tensor_tensor(gated[:, i % 2, :], silu[:, i % 2, :], bank[i % 2][:, INTER:2 * INTER],
                                      ALU.mult).then_inc(gated_ready, 1)
                shared_done[0] += n

            dve.wait_ge(prefix_ready, 1)
            done(dve.tensor_copy(chunk_count, work[1][:, 0:C * E].rearrange("p (c e) -> p e c", c=C)))
            settle()
            done(dve.tensor_tensor_scan(chunk_end.rearrange("p e c -> p (e c)"), not_first,
                                        chunk_count.rearrange("p e c -> p (e c)"), 0.0, ALU.mult, ALU.add))
            shared_gates(2)
            settle()
            done(dve.tensor_tensor(more_rows, chunk_end[:, :, C - 1:C].to_broadcast([P, E, E]),
                                   iota_rows.unsqueeze(1).to_broadcast([P, E, E]), ALU.is_gt))
            settle()
            done(dve.tensor_reduce(tiles_e[:, :], more_rows, AX.X, ALU.add))
            done(dve.tensor_tensor(chunk_end, chunk_end, chunk_count, ALU.subtract))
            settle()
            done(dve.tensor_tensor_scan(tile_end[:, :], ones[:, 0:E], tiles_e[:, :], 0.0, ALU.mult, ALU.add))
            settle()
            done(dve.tensor_tensor(row0[:, :], tile_end[:, :], tiles_e[:, :], ALU.subtract))
            settle()
            done(dve.tensor_scalar(row0[:, :], row0[:, :], float(P), None, ALU.mult))
            settle()
            done(dve.tensor_tensor(chunk_end, chunk_end, row0[:, :].unsqueeze(2).to_broadcast([P, E, C]), ALU.add))
            settle()
            done(dve.tensor_tensor(slot, work[0][:, 0:C * E].rearrange("p (c e) -> p c e", c=C),
                                   chunk_end.rearrange("p e c -> p c e"), ALU.add))
            settle()
            for k in range(2):
                done(dve.tensor_tensor(slot_k, slot, onehot[k], ALU.mult))
                settle()
                done(dve.tensor_reduce(slot_f[:, k, :], slot_k, AX.X, ALU.add))
                settle()
                dve.tensor_copy(slot_u[k][:, :], slot_f[:, k, :]).then_inc(slots_ready, 1)
            shared_gates(2)
            done(dve.tensor_tensor(past_end, tile_end[:, :].unsqueeze(1).to_broadcast([P, TILES, E]),
                                   iota_tile.unsqueeze(2).to_broadcast([P, TILES, E]), ALU.is_le))
            settle()
            done(dve.tensor_reduce(tile_ef[:, :], past_end, AX.X, ALU.add))
            settle()
            dve.tensor_scalar(tile_e[:, :], tile_ef[:, :], float(E - 1), None, ALU.min).then_inc(experts_ready, 1)

            def tile_in(at, i):
                dve.wait_ge(xt_ready, at(i + 1))
                dve.tensor_copy(tile_xT[:, i % 2].rearrange("p h t -> p (h t)"), work[i % 2][:, 0:D]).then_inc(xt_copied, 1)

            def tile_gate(at, i):
                dve.wait_ge(tsilu_ready, at(i + 1))
                dve.tensor_tensor(gated[:, i % 2, :], silu[:, i % 2, :], bank[i % 2][:, INTER:2 * INTER],
                                  ALU.mult).then_inc(tgated_ready, 1)

            def tile_out(at, i):
                if i >= LOADS:
                    dve.wait_ge(y_stored[i % LOADS], at.stored(i))
                dve.wait_ge(ty_ready, at(i + 1))
                dve.tensor_copy(tile_y[:, i % LOADS, :], ysum[i % 2][:, 0:D]).then_inc(ty_copied, 1)

            def tile_step(at, i):
                if i >= 0:
                    tile_gate(at, i)
                if i + 2 < TILES:
                    tile_in(at, i + 2)
                if i >= 1:
                    tile_out(at, i - 1)

            shared_gates(2 * SHARED_FIRST - shared_done[0])
            run_tiles(dve, tile_step)
            tile_out(Tile(), TILES - 1)
            for name, q in combine:
                if name == "gates":
                    shared_gates(2 * (SHARED_FIRST + q) - shared_done[0])
                elif name == "m_add":
                    dve.wait_ge(moe_copied, (q + 1) * CQ)
                    for j in range(CQ + 1):
                        for k, c in ((0, q * CQ + j), (1, q * CQ + j - 1)):
                            if not 0 <= c - q * CQ < CQ:
                                continue
                            if k == 0:
                                dve.wait_ge(y_gathered[c], 16 * 2)
                            else:
                                dve.wait_ge(dve_done, steps[0] - (j < CQ))
                            done(dve.scalar_tensor_tensor(f_moe[:, c, :], y_k[k][:, c, :], top8[:, c, k:k + 1],
                                                          f_moe[:, c, :], ALU.mult, ALU.add))
                    settle()
                elif name == "m_stat":
                    stat(f_moe, q)
                elif name == "m_norm":
                    scale(name, q)
                else:
                    for c in range(q * CQ, (q + 1) * CQ, 2):
                        dve.wait_ge(m_normed, c + 2)
                        dve.tensor_tensor(X[:, c:c + 2, :], X[:, c:c + 2, :], f_moe[:, c:c + 2, :], ALU.add).then_inc(out_ready, 1)

        @block.scalar
        def _(act):
            roots, norms = [0], [0]

            def root(q):
                g = slice(q * CQ, (q + 1) * CQ)
                roots[0] += 1
                act.wait_ge(var_ready, roots[0])
                act.activation(std[:, g], mom[:, g, 1], ACT.Sqrt, bias=eps_sb[:, 0:1]).then_inc(std_ready, 1)

            def normalise(name, q, l):
                norms[0] += 1
                act.wait_ge(scale_ready, norms[0])
                dst, src, signal = norm_of(name, l)
                for c in range(q * CQ, (q + 1) * CQ):
                    act.activation(dst[:, c, :], src[:, c, :], ACT.Identity, scale=rstd[:, c:c + 1], bias=shift[:, c:c + 1])\
                       .then_inc(signal, 1)

            def stage(name, q, l):
                g = slice(q * CQ, (q + 1) * CQ)
                t = slice(q * SEQ, (q + 1) * SEQ)
                k = l * Q + q
                if name in ("x_stat", "y_stat", "f_stat", "g_stat", "r_stat", "m_stat"):
                    root(q)
                elif name in ("y_add", "f_norm", "r_add", "m_norm"):
                    normalise(name, q, l)
                elif name == "turn":
                    for h in range(H):
                        act.wait_ge(tr_ready, k * H + h + 1)
                        act.activation(feat_a[:, h, t], work[h][:, :], ACT.Copy).then_inc(tr_copied, 1)
                elif name == "proj":
                    act.wait_ge(proj_ready, 2 * k + 1)
                    act.activation(dtpT[0:RANK[l], t], bank[0][0:RANK[l], :], ACT.Copy).then_inc(proj_copied, 1)
                    act.wait_ge(proj_ready, 2 * k + 2)
                    act.activation(bcT[:, t], bank[1][:, :], ACT.Copy).then_inc(bc_high, 1)
                elif name == "pre":
                    act.wait_ge(bc_rest, k + 1)
                    act.activation(bcT[64:P, t], state[64:P, q, :], ACT.Copy).then_inc(bc_mid, 1)
                    for h in range(H):
                        act.wait_ge(pre_ready, k * H + h + 1)
                        act.activation(dtT[:, h, t], bank[2 + h][:, :], ACT.Relu, bias=bdt_sb[l][:, h:h + 1])
                        act.activation(uT[:, h, t], bank[2 + h][:, :], ACT.Abs, bias=bdt_sb[l][:, h:h + 1])\
                           .then_inc(pre_used, 1)
                    for h in range(H):
                        act.wait_ge(pre_used, k * H + h + 1)
                        act.activation(uT[:, h, t], uT[:, h, t], ACT.Exp, scale=-1.0).then_inc(exp_ready, 1)
                elif name == "log":
                    for h in range(H):
                        act.wait_ge(err_ready, k * H + h + 1)
                        act.activation(w_buf[:, h, t], w_buf[:, h, t], ACT.Ln).then_inc(ln_ready, 1)
                elif name == "y_turn":
                    for j in range(2):
                        act.wait_ge(ytr_ready, ((l - 1) * Q + q) * 2 + j + 1)
                        act.activation(f_tok[l - 1][:, q * CQ + 2 * j:q * CQ + 2 * j + 2, :],
                                       bank[j][:, :].rearrange("p (c d) -> p c d", c=2), ACT.Copy).then_inc(ytr_copied, 1)
                elif name == "f_turn":
                    if q == 0:
                        act.wait_ge(fsign_in, 2)
                        act.activation(fw_sign[:, :, :], fw_sb[:, :, :], ACT.Sign).then_inc(fsign_out, 1)
                        act.wait_ge(fwT_ready, 1)
                        act.activation(fw_signT[:, :, :], bank[4][:, 0:D].bitcast(BF16).rearrange("p (h d) -> p h d", h=H),
                                       ACT.Copy).then_inc(fwT_copied, 1)
                        act.wait_ge(ld_ffn, 80)
                    for h in range(H):
                        act.wait_ge(ftr_ready, q * H + h + 1)
                        act.activation(a_signT[:, h, t], bank[2 + h][:, :], ACT.Sign, scale=gamma_sb[:, h:h + 1],
                                       bias=beta_sb[:, h:h + 1]).then_inc(ftr_copied, 1)
                elif name == "softmax":
                    act.wait_ge(sm_in, q + 1)
                    act.activation(probs[:, g, :], probs[:, g, :], ACT.Exp).then_inc(sm_out, 1)
                elif name == "f_back":
                    for j in range(2):
                        act.wait_ge(ftok_ready, q * 2 + j + 1)
                        act.activation(f_tok[0][:, q * CQ + 2 * j:q * CQ + 2 * j + 2, :],
                                       bank[j][:, :].rearrange("p (c d) -> p c d", c=2), ACT.Copy).then_inc(ftok_copied, 1)

            def scan(l):
                act.wait_ge(a_ready, l + 1)
                act.wait_ge(dt_ready, (l * BATCH + 1) * H)
                base = l * BATCH * UNITS
                nbase = l * BATCH * N

                def state_n(b, n, first):
                    if n >= CREP_RING or (n < AHEAD and not first):
                        act.wait_ge(hc_ready, b * UNITS + (base + H * (n - CREP_RING + 1)))
                    act.wait_ge(crep_ready, b * N + (nbase + n + 1))
                    for h in range(H):
                        u = n * H + h
                        part = slice(h * SEQ // H, (h + 1) * SEQ // H)
                        if not (first and u < ABAR_RING):
                            act.wait_ge(h_ready, b * UNITS + (base + u + 1 - ABAR_RING))
                        act.activation(crep[:, n % CREP_RING, part], cps[n % REP][:, part], ACT.Copy).then_inc(crep_copied, 1)
                        act.activation(abar[u % ABAR_RING][:, :], dtT[:, h, bass.ds(b * SEQ, SEQ)], ACT.Exp,
                                       scale=a_sb[l][:, h, n:n + 1]).then_inc(abar_ready, 1)

                def sequence(b, last):
                    for n in range(AHEAD, N):
                        state_n(b, n, False)
                    if not last:
                        for n in range(AHEAD):
                            state_n(b + 1, n, False)
                    act.wait_ge(state_free, b * UNITS + (base + UNITS + STATE_RING))
                    act.nop()
                    for h in range(H):
                        act.activation(yT[:, h, bass.ds(b * SEQ, SEQ)], ysum[h][:, :], ACT.Copy).then_inc(ysum_free, 1)

                for n in range(AHEAD):
                    state_n(0, n, True)
                act.wait_ge(dt_ready, (l + 1) * BATCH * H)
                with act.Fori(0, BATCH - 1) as b:
                    sequence(b, False)
                sequence(BATCH - 1, True)

            for name, q in in_turn(into_ssm):
                stage(name, q, 0)
            for l in range(2):
                act.wait_ge(ld_ssm[l], 80)
                act.activation(a_sb[l][:, :, :], a_sb[l][:, :, :], ACT.Exp).then_inc(a_exp_ready, 1)
            for name, q in in_turn(softplus):
                stage(name, q, 0)
            scan(0)
            for name, q in [*in_turn(out_of_ssm + ffn + into_ssm), *in_turn(softplus)]:
                stage(name, q, 1)
            scan(1)
            for name, q in in_turn(out_of_ssm + routing):
                stage(name, q, 2)

            def shared(lo, hi):
                for i in range(2 * lo, 2 * hi + 2):
                    if i < 2 * hi:
                        act.wait_ge(up_ready, i + 1)
                        act.activation(silu[:, i % 2, :], bank[i % 2][:, 0:INTER], ACT.Silu).then_inc(silu_ready, 1)
                    if 2 * lo <= i - 1 < 2 * hi:
                        act.wait_ge(gT_ready, i)
                        turned_out((i - 1) % 2).then_inc(gT_copied, 1)
                    c = (i - 2) // 2
                    if i % 2 and c >= lo:
                        act.wait_ge(moe_ready, c + 1)
                        act.activation(f_moe[:, c, :], ysum[c % 2][:, 0:D], ACT.Copy).then_inc(moe_copied, 1)

            def turned_out(k):
                act.activation(gatedT[:, k, 0, :], bank[2 + k][:, 0:P], ACT.Copy)
                return act.activation(gatedT[0:IR, k, 1, :], bank[2 + k][0:IR, P:2 * P], ACT.Copy)

            def tile_step(at, i):
                if 0 <= i + 1 < TILES:
                    act.wait_ge(tup_ready, at(i + 2))
                    act.activation(silu[:, (i + 1) % 2, :], bank[(i + 1) % 2][:, 0:INTER], ACT.Silu).then_inc(tsilu_ready, 1)
                if i >= 0:
                    act.wait_ge(tgT_ready, at(i + 1))
                    turned_out(i % 2).then_inc(tgT_copied, 1)

            shared(0, SHARED_FIRST)
            run_tiles(act, tile_step)
            shared(SHARED_FIRST, C)
            for name, q in combine:
                stage(name, q, 2)

        @block.gpsimd
        def _(pool):
            for l in range(2):
                pool.wait_ge(ld_ssm[l], 80)
                pool.tensor_copy(bcw_sb[l][:, :, :, :], win_sb[l][:, :, RANK[l]:].unsqueeze(2).to_broadcast([P, H, 4, 2 * N]))\
                    .then_inc(bcw_ready, 1)
            def product(l):
                base = l * BATCH * UNITS
                with pool.Fori(0, BATCH) as b:
                    for u in range(UNITS):
                        n, h = u // H, u % H
                        if h == 0:
                            pool.wait_ge(crep_copied, b * UNITS + (base + H * (n + 1)))
                        pool.wait_ge(h_ready, b * UNITS + (base + u + 1))
                        s = state[:, u % STATE_RING, :]
                        pool.tensor_tensor(s, s, crep[:, n % CREP_RING, :], ALU.mult).then_inc(hc_ready, 1)


            def stage(name, q, l):
                g = slice(q * CQ, (q + 1) * CQ)
                if name in ("y_add", "r_add"):
                    f, f_normed, x_added = (f_tok[l - 1], y_normed, y_added) if name == "y_add" else (f_tok[0], r_normed, r_added)
                    for c in range(q * CQ, (q + 1) * CQ):
                        n = ((l - 1) * C if name == "y_add" else 0) + c + 1
                        pool.wait_ge(f_normed, n)
                        pool.tensor_tensor(X[:, c, :], X[:, c, :], f[:, c, :], ALU.add).then_inc(x_added, 1)
                elif name == "dt":
                    k = l * Q + q
                    t = slice(q * SEQ, (q + 1) * SEQ)
                    pool.wait_ge(dt_ready, (k + 1) * H)
                    pool.tensor_tensor(uT[:, H - 1, t], dtT[:, H - 1, t], feat_a[:, H - 1, t], ALU.mult).then_inc(u_ready, 1)

            for name, q in [*in_turn(into_ssm), *in_turn(softplus)]:
                stage(name, q, 0)
            product(0)
            for name, q in [*in_turn(out_of_ssm + ffn + into_ssm), *in_turn(softplus)]:
                stage(name, q, 1)
            product(1)
            for name, q in in_turn(out_of_ssm + routing):
                stage(name, q, 2)
            pool.wait_ge(sorted_zeroed, 16)
            for k in range(2):
                pool.wait_ge(slots_ready, k + 1)
                for c in range(C):
                    pool.indirect_dma_start(out=x_sorted, out_offset=bass.IndirectOffsetOnAxis(ap=slot_u[k][:, c:c + 1], axis=0),
                                            in_=tok_a[:, c, :], in_offset=None).then_inc(sorted_ready, 16)
            pool.wait_ge(sorted_ready, 16 * 2 * C)
            for k in range(LOADS):
                pool.wait_ge(y_stored[k], 16 * len(range(k, TILES, LOADS)))
            for q in range(Q):
                for c in range(q * CQ, (q + 1) * CQ):
                    for k in range(2):
                        pool.indirect_dma_start(out=y_k[k][:, c, :], out_offset=None, in_=y_sorted,
                                                in_offset=bass.IndirectOffsetOnAxis(ap=slot_u[k][:, c:c + 1], axis=0))\
                            .then_inc(y_gathered[c], 16)

        @block.tensor
        def _(pe):
            def stage(name, q, l):
                t = slice(q * SEQ, (q + 1) * SEQ)
                k = l * Q + q
                if name == "turn":
                    pe.wait_ge(norm_ready, (k + 1) * CQ)
                    if k:
                        pe.wait_ge(tr_copied, k * H)
                    for h in range(H):
                        for j in range(CQ):
                            ins = pe.transpose(work[h][:, j * P:(j + 1) * P], tok_a[:, q * CQ + j, h * P:(h + 1) * P],
                                               ident[:, :])
                        ins.then_inc(tr_ready, 1)
                elif name == "proj":
                    r = RANK[l]
                    if q == 0:
                        pe.wait_ge(ld_ssm[l], 80)
                        pe.wait_ge(bcw_ready, l + 1)
                        if l:
                            pe.wait_ge(ftok_copied, Q * 2)
                    if k:
                        pe.wait_ge(proj_copied, k)
                        pe.wait_ge(bc_rest, k)
                    pe.wait_ge(tr_copied, (k + 1) * H)
                    for h in range(H):
                        ins = pe.matmul(bank[0][0:r, :], win_sb[l][:, h, 0:r], feat_a[:, h, t], start=h == 0, stop=h == H - 1)
                    ins.then_inc(proj_ready, 1)
                    for h in range(H):
                        ins = pe.matmul(bank[1][:, :], bcw_sb[l][:, h].rearrange("p k j -> p (k j)"), feat_a[:, h, t],
                                        start=h == 0, stop=h == H - 1)
                    ins.then_inc(proj_ready, 1)
                elif name == "pre":
                    pe.wait_ge(proj_copied, k + 1)
                    if l and q == 0:
                        pe.wait_ge(ftr_copied, Q * H)
                    if k:
                        pe.wait_ge(pre_used, k * H)
                    for h in range(H):
                        pe.matmul(bank[2 + h][:, :], wdt_sb[l][:, h * P:(h + 1) * P], dtpT[0:RANK[l], t],
                                  start=True, stop=True).then_inc(pre_ready, 1)
                elif name == "gate":
                    if q == 0:
                        pe.wait_ge(ld_gate, 48)
                    pe.wait_ge(tr_copied, (k + 1) * H)
                    for j in range(CQ):
                        c = q * CQ + j
                        for h in range(H):
                            ins = pe.matmul(logits[q][:, j, :], feat_a[:, h, c * P:(c + 1) * P], gatew_sb[:, h, :],
                                            start=h == 0, stop=h == H - 1)
                    ins.then_inc(gate_ready, 1)
                elif name == "y_turn":
                    pe.wait_ge(ysum_free, H + ((l - 1) * BATCH + q + 1) * H)
                    if q:
                        pe.wait_ge(ytr_copied, ((l - 1) * Q + q) * H)
                    for j in range(2):
                        for i in range(2):
                            c = q * CQ + 2 * j + i
                            for h in range(H):
                                ins = pe.transpose(bank[j][:, (i * H + h) * P:(i * H + h + 1) * P],
                                                   yT[:, h, c * P:(c + 1) * P], ident[:, :])
                        ins.then_inc(ytr_ready, 1)
                elif name == "f_turn":
                    if q == 0:
                        pe.wait_ge(fsign_out, 1)
                        for i in range(H):
                            for h in range(H):
                                o = bank[4][:, 0:D].bitcast(BF16)[:, i * D + h * P:i * D + (h + 1) * P]
                                ins = pe.transpose(o, fw_sign[:, h, i * P:(i + 1) * P], ident_bf[:, :])
                        ins.then_inc(fwT_ready, 1)
                    pe.wait_ge(g_normed, (q + 1) * CQ)
                    if q:
                        pe.wait_ge(ftr_copied, q * H)
                    for h in range(H):
                        for j in range(CQ):
                            ins = pe.transpose(bank[2 + h][:, j * P:(j + 1) * P], tok_a[:, q * CQ + j, h * P:(h + 1) * P],
                                               ident[:, :])
                        ins.then_inc(ftr_ready, 1)
                elif name == "f_mm":
                    if q == 0:
                        pe.wait_ge(fwT_copied, 1)
                    else:
                        pe.wait_ge(scaled, q * H)
                    pe.wait_ge(ftr_copied, (q + 1) * H)
                    for i in range(H):
                        for h in range(H):
                            ins = pe.matmul(bank[4 + i][:, :], fw_signT[:, h, i * P:(i + 1) * P], a_signT[:, h, t],
                                            start=h == 0, stop=h == H - 1)
                        ins.then_inc(ffn_ready, 1)
                elif name == "f_back":
                    pe.wait_ge(scaled, (q + 1) * H)
                    pe.wait_ge(ytr_copied if q == 0 else ftok_copied, Q * 2 if q == 0 else q * 2)
                    for j in range(2):
                        for i in range(2):
                            c = q * CQ + 2 * j + i
                            for h in range(H):
                                ins = pe.transpose(bank[j][:, (i * H + h) * P:(i * H + h + 1) * P],
                                                   feat_a[:, h, c * P:(c + 1) * P], ident[:, :])
                        ins.then_inc(ftok_ready, 1)

            def scan(l):
                base, nbase = l * BATCH * UNITS, l * BATCH * N
                pe.wait_ge(bc_ready, (l + 1) * BATCH)
                pe.wait_ge(ddiag_ready, l + 1)
                pe.wait_ge(pre_used, (l + 1) * BATCH * H)

                def replicate(b, n, first=False):
                    rhs = bcT[:, bass.ds(b * SEQ, SEQ)]
                    if not first:
                        pe.wait_ge(b_ready, b * UNITS + (base + H * (n + 1 - REP)))
                    pe.matmul(brep[n % REP][:, :], spread_bf[:, n:n + 1].to_broadcast([P, P]), rhs,
                              start=True, stop=True).then_inc(brep_ready, 1)
                    if not first:
                        pe.wait_ge(crep_copied, b * UNITS + (base + H * (n + 1 - REP)))
                    pe.matmul(cps[n % REP][:, :], spread_bf[:, N + n:N + n + 1].to_broadcast([P, P]), rhs,
                              start=True, stop=True).then_inc(crep_ready, 1)

                def sequence(b, last):
                    for n in range(N):
                        if n + REP < N:
                            replicate(b, n + REP)
                        elif not last:
                            replicate(b + 1, n + REP - N)
                        for h in range(H):
                            u = n * H + h
                            if n == 0:
                                pe.wait_ge(ysum_free, b * H + (l * BATCH * H + h + 1))
                            pe.wait_ge(hc_ready, b * UNITS + (base + u + 1))
                            pe.matmul(ysum[h][:, :], ident[:, :], state[:, u % STATE_RING, :], start=n == 0,
                                      stop=n == N - 1).then_inc(state_free, 1)
                        if N // 2 <= n < N // 2 + H:
                            h = n - N // 2
                            pe.matmul(ysum[h][:, :], ddiag[:, h, :], feat_a[:, h, bass.ds(b * SEQ, SEQ)], start=False, stop=False)

                for n in range(REP):
                    replicate(0, n, True)
                with pe.Fori(0, BATCH - 1) as b:
                    sequence(b, False)
                sequence(BATCH - 1, True)

            pe.sem_inc(state_free, STATE_RING)
            pe.sem_inc(ysum_free, H)
            pe.wait_ge(ld_ident, 16)
            for name, q in [*in_turn(into_ssm), *in_turn(softplus)]:
                stage(name, q, 0)
            scan(0)
            for name, q in [*in_turn(out_of_ssm + ffn + into_ssm), *in_turn(softplus)]:
                stage(name, q, 1)
            scan(1)
            for name, q in in_turn(out_of_ssm + routing):
                stage(name, q, 2)
            def up(xT, e, k):
                for h in range(H):
                    ins = pe.matmul(bank[k][:, 0:2 * INTER], xT[h], w13_sb[:, h, e, :], start=h == 0, stop=h == H - 1)
                return ins

            def turn(k):
                pe.transpose(bank[2 + k][:, 0:P], gated[:, k, 0:P], ident[:, :])
                return pe.transpose(bank[2 + k][0:IR, P:2 * P], gated[:, k, P:INTER], ident[:, :])

            def down(o, e, k, first, last):
                pe.matmul(ysum[o][:, 0:D], gatedT[:, k, 0, :], w2a[:, e, :], start=first, stop=False)
                return pe.matmul(ysum[o][:, 0:D], gatedT[0:IR, k, 1, :], w2b[:, e, :], start=False, stop=last)

            def expert_rows():
                pe.wait_ge(onehot_ready, Q)
                flat = picked.rearrange("p c e -> p (c e)")
                pe.matmul(work[0][:, 0:C * E], upper_sb[:, :], flat, start=True, stop=True)
                pe.matmul(work[1][:, 0:C * E], ones[:, :], flat, start=True, stop=True).then_inc(prefix_ready, 1)

            def shared(lo, hi):
                for i in range(2 * lo, 2 * hi + 2):
                    if i < 2 * hi:
                        if i >= 2:
                            pe.wait_ge(gated_ready, i - 1)
                        c = i // 2
                        up([feat_a[:, h, c * P:(c + 1) * P] for h in range(H)], E + i % 2, i % 2).then_inc(up_ready, 1)
                    if i == 1:
                        expert_rows()
                    if 2 * lo <= i - 1 < 2 * hi:
                        pe.wait_ge(gated_ready, i)
                        turn((i - 1) % 2).then_inc(gT_ready, 1)
                    if i - 2 >= 2 * lo:
                        j = i - 2
                        c = j // 2
                        pe.wait_ge(gT_copied, j + 1)
                        if j % 2 == 0 and c >= 2:
                            pe.wait_ge(moe_copied, c - 1)
                        ins = down(c % 2, E + j % 2, j % 2, j % 2 == 0, j % 2 == 1)
                        if j % 2:
                            ins.then_inc(moe_ready, 1)

            expert_reg = [pe.alloc_register(f"expert{k}") for k in range(LOADS)]

            def expert(i):
                return pe.snap(expert_reg[i % LOADS], min_val=0, max_val=E - 1)

            def tile_step(at, i):
                if 0 <= i + 1 < TILES:
                    pe.reg_load(expert_reg[(i + 1) % LOADS], tile_e[0:1, at.slice(i + 1)])
                if i + 2 < TILES:
                    j = i + 2
                    pe.wait_ge(x_loaded[j % LOADS], at.loaded(j))
                    for h in range(H):
                        if h and i >= 3:
                            pe.wait_ge(ty_copied, at(i - 2))
                        ins = pe.transpose(work[j % 2][:, h * P:(h + 1) * P], tile_x[:, j % LOADS, h * P:(h + 1) * P], ident[:, :])
                    ins.then_inc(xt_ready, 1)
                if 0 <= i + 1 < TILES:
                    pe.wait_ge(xt_copied, at(i + 2))
                    up([tile_xT[:, (i + 1) % 2, h, :] for h in range(H)], bass.ds(expert(i + 1), 1), (i + 1) % 2).then_inc(tup_ready, 1)
                if i >= 0:
                    pe.wait_ge(tgated_ready, at(i + 1))
                    turn(i % 2).then_inc(tgT_ready, 1)
                if i >= 1:
                    tile_down(at, i - 1)

            def tile_down(at, i):
                if i >= TILES - 3:
                    pe.wait_ge(ty_copied, i - 1)
                pe.wait_ge(tgT_copied, at(i + 1))
                down(i % 2, bass.ds(expert(i), 1), i % 2, True, True).then_inc(ty_ready, 1)

            pe.wait_ge(ld_w13, 16 * H)
            pe.wait_ge(ld_w2, 32)
            shared(0, SHARED_FIRST)
            pe.wait_ge(moe_copied, SHARED_FIRST)
            pe.wait_ge(experts_ready, 1)
            run_tiles(pe, tile_step)
            tile_down(Tile(), TILES - 1)
            pe.wait_ge(ty_copied, TILES)
            shared(SHARED_FIRST, C)


def in_turn(stages):
    for step in range(len(stages) + Q - 1):
        for q in reversed(range(Q)):
            if 0 <= step - q < len(stages):
                yield stages[step - q], q


class Tile:

    def __init__(self, m=None):
        self.m = m

    def __call__(self, i):
        return i if self.m is None else self.m * LOADS + i

    def loaded(self, i):
        n = 16 * (i // LOADS + 1)
        return n if self.m is None else self.m * 16 + n

    def stored(self, i):
        n = 16 * (i // LOADS)
        return n if self.m is None else self.m * 16 + n

    def slice(self, i):
        return slice(i, i + 1) if self.m is None else bass.ds(self.m * LOADS + i, 1)


def run_tiles(engine, step):
    first = LOADS + 2
    rounds = (TILES - 2 - first) // LOADS
    for i in range(-2, first):
        step(Tile(), i)
    with engine.Fori(0, rounds) as m:
        for k in range(LOADS):
            step(Tile(m), first + k)
    for i in range(first + rounds * LOADS, TILES):
        step(Tile(), i)


def kernel(**inputs):
    import numpy as np
    import concourse.bacc as bacc
    from concourse import mybir as mb
    from concourse.bass_utils import run_bass_kernel_spmd as launch

    i = {k: np.asarray(v) for k, v in inputs.items()}
    sw1, sw3 = (i[f"L1_ffn_{n}"].reshape(ES - E, INTER, D) for n in ("sw1", "sw3"))
    sw2 = i["L1_ffn_sw2"].reshape(D, ES - E, INTER).transpose(1, 0, 2)
    w1, w3, w2 = (np.concatenate([i[f"L1_ffn_{n}"], s]) for n, s in (("w1", sw1), ("w3", sw3), ("w2", sw2)))
    arrays = {
        "x": i["L0_attn_x"].reshape(T, D),
        "eye": np.eye(P, dtype=np.float32),
        "spread": np.concatenate([np.eye(2 * N), 0 * np.eye(2 * N), np.eye(2 * N), np.eye(2 * N)]).astype(np.float32),
        "a_log0": i["L0_attn_A_log"], "a_log1": i["L1_attn_A_log"],
        "d_skip0": i["L0_attn_D"].reshape(H, P).T, "d_skip1": i["L1_attn_D"].reshape(H, P).T,
        "w_in0": i["L0_attn_W_xproj"].T,
        "w_in1": np.concatenate([i["L1_attn_W_delta"], i["L1_attn_W_B"], i["L1_attn_W_C"]], axis=1),
        "w_dt0": i["L0_attn_W_dt"].T, "w_dt1": i["L1_attn_W_dt"],
        "b_dt0": i["L0_attn_b_dt"].reshape(H, P).T, "b_dt1": i["L1_attn_b_dt"].reshape(H, P).T,
        "weight": i["L0_ffn_weight"],
        **{n: i[f"L0_ffn_{n}"].reshape(H, P).T for n in ("gamma", "beta", "bias", "alpha")},
        "gate_wt": i["L1_ffn_gate_w"].T, "upper": np.triu(np.ones((P, P), np.float32), 1),
        "counts": np.concatenate([np.arange(E), P * np.arange(E), np.arange(TILES),
                                  np.arange(E * C) % C != 0]).astype(np.float32),
        "w13": np.concatenate([w1, w3], axis=1).transpose(0, 2, 1), "w2": w2.transpose(0, 2, 1),
    }
    arrays = {k: np.ascontiguousarray(v) for k, v in arrays.items()}
    nc = bacc.Bacc("TRN2", target_bir_lowering=False, num_devices=1)
    ap = {k: nc.dram_tensor(k, v.shape, mb.dt.from_np(v.dtype), kind="ExternalInput").ap() for k, v in arrays.items()}
    for k in ("a_log", "d_skip", "w_in", "w_dt", "b_dt"):
        ap[k] = [ap.pop(f"{k}{l}") for l in range(2)]
    ap["out"] = nc.dram_tensor("out", (T, D), F32, kind="ExternalOutput").ap()
    for k in ("x_sorted", "y_sorted"):
        ap[k] = nc.dram_tensor(k, (TILES * P, D), F32, kind="Internal").ap()
    sandwich_kernel(nc, **ap)
    r = launch(nc, [arrays], core_ids=[0])
    return r.results[0]["out"].reshape(BATCH, SEQ, D)
```
